# Optimizing a Trainium2 kernel written in Bass

```python
import numpy as np
import jax
import jax.numpy as jnp

def _softmax(x, axis=-1):
    return jax.nn.softmax(x, axis=axis)

def _gelu(x):
    return jax.nn.gelu(x, approximate=True)

def _silu(x):
    return jax.nn.silu(x)

def _sigmoid(x):
    return jax.nn.sigmoid(x)

def _layernorm(x, axis=-1, eps=1e-05):
    m = jnp.mean(x, axis=axis, keepdims=True)
    v = jnp.var(x, axis=axis, keepdims=True)
    return (x - m) / jnp.sqrt(v + eps)

def _scatter_add(tgt, idx, src, axis=0):
    return tgt.at[idx].add(src)

def _segment_sum(src, seg, n):
    return jax.ops.segment_sum(src, seg, n)
kernel_name = 'mk_gnn_resnorm_d4_gnn_r16_8f65f5'

def setup_inputs(seed: int=0):
    np.random.seed(seed)
    _w = jnp.asarray

    def _rec_inputs():
        import jax
        import jax.numpy as jnp
        _gk = jax.random.key(seed)
        x = -0.0003713 + 1 * jax.random.normal(jax.random.fold_in(_gk, 1), (6250, 256), jnp.float32)
        _s = jax.random.randint(jax.random.fold_in(_gk, 2), (50000,), 0, 6250, jnp.int32)
        _d = jax.random.randint(jax.random.fold_in(_gk, 3), (50000,), 0, 6250, jnp.int32)
        _loop = jnp.arange(6250, dtype=jnp.int32)
        src = jnp.concatenate([_s, _d, _loop])
        dst = jnp.concatenate([_d, _s, _loop])
        _o = jnp.argsort(dst, stable=True)
        src = src[_o]
        dst = dst[_o]
        edge_type_16 = jax.random.randint(jax.random.fold_in(_gk, 14), (106250,), 0, 16, jnp.int32)
        edge_type_32 = jax.random.randint(jax.random.fold_in(_gk, 15), (106250,), 0, 32, jnp.int32)
        edge_weight1 = jax.random.uniform(jax.random.fold_in(_gk, 16), (106250, 1), jnp.float32, 0.0, 0.999998)
        return (x, src, dst, edge_type_16, edge_type_32, edge_weight1)
    x, src, dst, edge_type_16, edge_type_32, edge_weight1 = _rec_inputs()

    def _L0_gnn_setup():
        import jax, jax.numpy as jnp
        import numpy as np
        N_NODES = 3125
        N_EDGES = 50000
        D_IN = 256
        D_OUT = 256
        BN_EPS = 1e-05
        L2_EPS = 1e-12
        key = jax.random.key(seed)
        ks = jax.random.split(key, 8)
        x = jax.random.normal(ks[0], (N_NODES, D_IN), dtype=jnp.float32)
        edge_index = jax.random.randint(ks[1], (2, N_EDGES), 0, N_NODES, dtype=jnp.int64)
        s = 1.0 / np.sqrt(D_IN)
        W_l = jax.random.uniform(ks[2], (D_OUT, D_IN), jnp.float32, -s, s)
        b_l = jax.random.uniform(ks[3], (D_OUT,), jnp.float32, -s, s)
        W_r = jax.random.uniform(ks[4], (D_OUT, D_IN), jnp.float32, -s, s)
        gamma = jnp.ones((D_OUT,), jnp.float32)
        beta = jnp.zeros((D_OUT,), jnp.float32)
        return {'x': x, 'edge_index': edge_index, 'W_l': W_l, 'b_l': b_l, 'W_r': W_r, 'gamma': gamma, 'beta': beta}
    _L0_gnn_all = _L0_gnn_setup()
    _L0_gnn_in = {k: v for k, v in _L0_gnn_all.items() if k in ('W_l', 'b_l', 'W_r', 'gamma', 'beta')}
    del _L0_gnn_all

    def _L1_gnn_setup():
        import jax, jax.numpy as jnp
        import numpy as np
        N_NODES = 3125
        N_EDGES = 50000
        HDIM = 256
        NUMRELS = 16

        def _gru_cell(x, h, w_ih, w_hh, b_ih, b_hh):
            gi = x @ w_ih.T + b_ih
            gh = h @ w_hh.T + b_hh
            i_r, i_z, i_n = jnp.split(gi, 3, axis=-1)
            h_r, h_z, h_n = jnp.split(gh, 3, axis=-1)
            r = jax.nn.sigmoid(i_r + h_r)
            z = jax.nn.sigmoid(i_z + h_z)
            n = jnp.tanh(i_n + r * h_n)
            return (1.0 - z) * n + z * h
        key = jax.random.key(seed)
        ks = jax.random.split(key, 9)
        h = jax.random.normal(ks[0], (N_NODES, HDIM), dtype=jnp.float32)
        relvectors = jax.random.normal(ks[1], (NUMRELS, HDIM), dtype=jnp.float32)
        s = 1.0 / np.sqrt(HDIM)
        w_ih = jax.random.uniform(ks[2], (3 * HDIM, HDIM), minval=-s, maxval=s, dtype=jnp.float32)
        w_hh = jax.random.uniform(ks[3], (3 * HDIM, HDIM), minval=-s, maxval=s, dtype=jnp.float32)
        b_ih = jax.random.uniform(ks[4], (3 * HDIM,), minval=-s, maxval=s, dtype=jnp.float32)
        b_hh = jax.random.uniform(ks[5], (3 * HDIM,), minval=-s, maxval=s, dtype=jnp.float32)
        edge_src = jax.random.randint(ks[6], (N_EDGES,), 0, N_NODES, dtype=jnp.int32)
        edge_dst = jax.random.randint(ks[7], (N_EDGES,), 0, N_NODES, dtype=jnp.int32)
        edge_rel = jax.random.randint(ks[8], (N_EDGES,), 0, NUMRELS, dtype=jnp.int32)
        return {'h': h, 'relvectors': relvectors, 'w_ih': w_ih, 'w_hh': w_hh, 'b_ih': b_ih, 'b_hh': b_hh, 'edge_src': edge_src, 'edge_dst': edge_dst, 'edge_rel': edge_rel}
    _L1_gnn_all = _L1_gnn_setup()
    _L1_gnn_in = {k: v for k, v in _L1_gnn_all.items() if k in ('relvectors', 'w_ih', 'w_hh', 'b_ih', 'b_hh')}
    del _L1_gnn_all

    def _L2_gnn_setup():
        import jax, jax.numpy as jnp
        import numpy as np
        N_NODES = 1250
        N_EDGES = 20000
        IN_DIM = 256
        OUT_DIM = 256
        NUM_RELS = 32
        NUM_BASES = 8
        key = jax.random.key(seed)
        k1, k2, k3, k4, k5, k6, k7 = jax.random.split(key, 7)
        h = jax.random.normal(k1, (N_NODES, IN_DIM), dtype=jnp.float32)
        src = jax.random.randint(k2, (N_EDGES,), 0, N_NODES, dtype=jnp.int32)
        dst = jax.random.randint(k3, (N_EDGES,), 0, N_NODES, dtype=jnp.int32)
        rel_type = jax.random.randint(k4, (N_EDGES,), 0, NUM_RELS, dtype=jnp.int32)
        norm = jax.random.uniform(k5, (N_EDGES, 1), dtype=jnp.float32)
        scale_w = np.sqrt(2.0) * np.sqrt(6.0 / (IN_DIM + OUT_DIM))
        bases = jax.random.uniform(k6, (NUM_BASES, IN_DIM, OUT_DIM), dtype=jnp.float32, minval=-scale_w, maxval=scale_w)
        scale_c = np.sqrt(2.0) * np.sqrt(6.0 / (NUM_RELS + NUM_BASES))
        w_comp = jax.random.uniform(k7, (NUM_RELS, NUM_BASES), dtype=jnp.float32, minval=-scale_c, maxval=scale_c)
        return {'h': h, 'src': src, 'dst': dst, 'rel_type': rel_type, 'norm': norm, 'bases': bases, 'w_comp': w_comp}
    _L2_gnn_all = _L2_gnn_setup()
    _L2_gnn_in = {k: v for k, v in _L2_gnn_all.items() if k in ('bases', 'w_comp')}
    del _L2_gnn_all

    def _L3_gnn_setup():
        import jax, jax.numpy as jnp
        import numpy as np
        V = 1024
        G = 32
        D = 256
        N = 8
        H = 32
        I = 1024
        LN_EPS = 1e-12

        def _layer_norm(x, g, b):
            mu = jnp.mean(x, axis=-1, keepdims=True)
            var = jnp.mean(jnp.square(x - mu), axis=-1, keepdims=True)
            return (x - mu) * jax.lax.rsqrt(var + LN_EPS) * g + b
        key = jax.random.key(seed)
        ks = jax.random.split(key, 5)
        node_embeddings = jax.random.normal(ks[0], (V, D), jnp.float32)
        idx = np.arange(V, dtype=np.int32).reshape(-1, G)
        src = np.repeat(idx, G, axis=1).reshape(-1)
        dst = np.tile(idx, (1, G)).reshape(-1)
        in_graph_node_pairs = jnp.asarray(np.stack([src, dst], axis=-1))
        s = 0.02
        return {'node_embeddings': node_embeddings, 'in_graph_node_pairs': in_graph_node_pairs, 'W_qkv': jax.random.normal(ks[1], (D, 3 * N * H), jnp.float32) * s, 'W_o': jax.random.normal(ks[2], (N * H, D), jnp.float32) * s, 'ln1_g': jnp.ones((D,), jnp.float32), 'ln1_b': jnp.zeros((D,), jnp.float32), 'W_i': jax.random.normal(ks[3], (D, I), jnp.float32) * s, 'W_out2': jax.random.normal(ks[4], (I, D), jnp.float32) * s, 'ln2_g': jnp.ones((D,), jnp.float32), 'ln2_b': jnp.zeros((D,), jnp.float32)}
    _L3_gnn_all = _L3_gnn_setup()
    _L3_gnn_in = {k: v for k, v in _L3_gnn_all.items() if k in ('W_qkv', 'W_o', 'ln1_g', 'ln1_b', 'W_i', 'W_out2', 'ln2_g', 'ln2_b')}
    del _L3_gnn_all
    return {'x': x, 'src': src, 'dst': dst, 'edge_type_16': edge_type_16, 'edge_type_32': edge_type_32, 'edge_weight1': edge_weight1, 'L0_gnn_W_l': _L0_gnn_in['W_l'], 'L0_gnn_b_l': _L0_gnn_in['b_l'], 'L0_gnn_W_r': _L0_gnn_in['W_r'], 'L0_gnn_gamma': _L0_gnn_in['gamma'], 'L0_gnn_beta': _L0_gnn_in['beta'], 'L1_gnn_relvectors': _L1_gnn_in['relvectors'], 'L1_gnn_w_ih': _L1_gnn_in['w_ih'], 'L1_gnn_w_hh': _L1_gnn_in['w_hh'], 'L1_gnn_b_ih': _L1_gnn_in['b_ih'], 'L1_gnn_b_hh': _L1_gnn_in['b_hh'], 'L2_gnn_bases': _L2_gnn_in['bases'], 'L2_gnn_w_comp': _L2_gnn_in['w_comp'], 'L3_gnn_W_qkv': _L3_gnn_in['W_qkv'], 'L3_gnn_W_o': _L3_gnn_in['W_o'], 'L3_gnn_ln1_g': _L3_gnn_in['ln1_g'], 'L3_gnn_ln1_b': _L3_gnn_in['ln1_b'], 'L3_gnn_W_i': _L3_gnn_in['W_i'], 'L3_gnn_W_out2': _L3_gnn_in['W_out2'], 'L3_gnn_ln2_g': _L3_gnn_in['ln2_g'], 'L3_gnn_ln2_b': _L3_gnn_in['ln2_b']}

def reference(x, src, dst, edge_type_16, edge_type_32, edge_weight1, L0_gnn_W_l, L0_gnn_b_l, L0_gnn_W_r, L0_gnn_gamma, L0_gnn_beta, L1_gnn_relvectors, L1_gnn_w_ih, L1_gnn_w_hh, L1_gnn_b_ih, L1_gnn_b_hh, L2_gnn_bases, L2_gnn_w_comp, L3_gnn_W_qkv, L3_gnn_W_o, L3_gnn_ln1_g, L3_gnn_ln1_b, L3_gnn_W_i, L3_gnn_W_out2, L3_gnn_ln2_g, L3_gnn_ln2_b):
    import jax
    import jax.numpy as jnp

    def _L0_gnn_ref(x, edge_index, W_l, b_l, W_r, gamma, beta):
        import jax, jax.numpy as jnp
        import numpy as np
        N_NODES = 3125
        N_EDGES = 50000
        D_IN = 256
        D_OUT = 256
        BN_EPS = 1e-05
        L2_EPS = 1e-12
        N = x.shape[0]
        src = edge_index[0]
        dst = edge_index[1]
        agg = jax.ops.segment_sum(x[src], dst, num_segments=N)
        deg = jax.ops.segment_sum(jnp.ones_like(src, dtype=x.dtype), dst, num_segments=N)
        mean = agg / jnp.maximum(deg, 1.0)[:, None]
        out = mean @ W_l.T + b_l + x @ W_r.T
        nrm = jnp.sqrt(jnp.sum(out * out, axis=-1, keepdims=True))
        out = out / jnp.maximum(nrm, L2_EPS)
        mu = jnp.mean(out, axis=0)
        var = jnp.mean((out - mu) ** 2, axis=0)
        out = (out - mu) / jnp.sqrt(var + BN_EPS) * gamma + beta
        return jax.nn.relu(out)

    def _L1_gnn_ref(h, relvectors, w_ih, w_hh, b_ih, b_hh, edge_src, edge_dst, edge_rel):
        import jax, jax.numpy as jnp
        import numpy as np
        N_NODES = 3125
        N_EDGES = 50000
        HDIM = 256
        NUMRELS = 16

        def _gru_cell(x, h, w_ih, w_hh, b_ih, b_hh):
            gi = x @ w_ih.T + b_ih
            gh = h @ w_hh.T + b_hh
            i_r, i_z, i_n = jnp.split(gi, 3, axis=-1)
            h_r, h_z, h_n = jnp.split(gh, 3, axis=-1)
            r = jax.nn.sigmoid(i_r + h_r)
            z = jax.nn.sigmoid(i_z + h_z)
            n = jnp.tanh(i_n + r * h_n)
            return (1.0 - z) * n + z * h
        msg = h[edge_src] + relvectors[edge_rel]
        red = jax.ops.segment_sum(msg, edge_dst, num_segments=h.shape[0])
        return _gru_cell(red, h, w_ih, w_hh, b_ih, b_hh)

    def _L2_gnn_ref(h, src, dst, rel_type, norm, bases, w_comp):
        import jax, jax.numpy as jnp
        import numpy as np
        N_NODES = 1250
        N_EDGES = 20000
        IN_DIM = 256
        OUT_DIM = 256
        NUM_RELS = 32
        NUM_BASES = 8
        weight = jnp.einsum('rb,bio->rio', w_comp, bases)
        xw = jnp.einsum('ni,rio->nro', h, weight)
        msg = xw[src, rel_type] * norm
        out = jax.ops.segment_sum(msg, dst, num_segments=h.shape[0])
        return jax.nn.relu(out)

    def _L3_gnn_ref(node_embeddings, in_graph_node_pairs, W_qkv, W_o, ln1_g, ln1_b, W_i, W_out2, ln2_g, ln2_b):
        import jax, jax.numpy as jnp
        import numpy as np
        V = 1024
        G = 32
        D = 256
        N = 8
        H = 32
        I = 1024
        LN_EPS = 1e-12

        def _layer_norm(x, g, b):
            mu = jnp.mean(x, axis=-1, keepdims=True)
            var = jnp.mean(jnp.square(x - mu), axis=-1, keepdims=True)
            return (x - mu) * jax.lax.rsqrt(var + LN_EPS) * g + b
        nV = node_embeddings.shape[0]
        src = in_graph_node_pairs[:, 0]
        dst = in_graph_node_pairs[:, 1]
        qkv = (node_embeddings @ W_qkv).reshape(nV, N, 3 * H)
        q, k, v = jnp.split(qkv, 3, axis=-1)
        scores = jnp.einsum('phi,phi->ph', q[src], k[dst]) / jnp.sqrt(jnp.float32(H))
        m = jax.ops.segment_max(scores, src, num_segments=nV)
        e = jnp.exp(scores - m[src])
        denom = jax.ops.segment_sum(e, src, num_segments=nV)
        w = e / denom[src]
        wv = w[:, :, None] * v[dst]
        att = jax.ops.segment_sum(wv, src, num_segments=nV).reshape(nV, N * H)
        pre = _layer_norm(att @ W_o + node_embeddings, ln1_g, ln1_b)
        inter = jax.nn.gelu(pre @ W_i, approximate=False)
        out = _layer_norm(inter @ W_out2 + pre, ln2_g, ln2_b)
        return out
    edge_index = jnp.stack([src, dst])
    edge_index_t = jnp.stack([src, dst], axis=1)
    x = _layernorm(x + _L0_gnn_ref(x, edge_index, L0_gnn_W_l, L0_gnn_b_l, L0_gnn_W_r, L0_gnn_gamma, L0_gnn_beta), axis=-1)
    x = _layernorm(x + _L1_gnn_ref(x, L1_gnn_relvectors, L1_gnn_w_ih, L1_gnn_w_hh, L1_gnn_b_ih, L1_gnn_b_hh, src, dst, edge_type_16), axis=-1)
    x = _layernorm(x + _L2_gnn_ref(x, src, dst, edge_type_32, edge_weight1, L2_gnn_bases, L2_gnn_w_comp), axis=-1)
    x = _layernorm(x + _L3_gnn_ref(x, edge_index_t, L3_gnn_W_qkv, L3_gnn_W_o, L3_gnn_ln1_g, L3_gnn_ln1_b, L3_gnn_W_i, L3_gnn_W_out2, L3_gnn_ln2_g, L3_gnn_ln2_b), axis=-1)
    return x

_drawn_inputs = setup_inputs


def setup_inputs(seed=0):
    import zlib

    import numpy as np

    out = dict(_drawn_inputs(seed))
    spreads = {'L0_gnn_gamma': (1.0, 0.2),
     'L0_gnn_beta': (0.0, 0.1),
     'L3_gnn_ln1_g': (1.0, 0.2),
     'L3_gnn_ln1_b': (0.0, 0.1),
     'L3_gnn_ln2_g': (1.0, 0.2),
     'L3_gnn_ln2_b': (0.0, 0.1)}
    factors = {'L0_gnn_b_l': 8.0,
     'L1_gnn_b_ih': 7.946,
     'L1_gnn_b_hh': 8.0,
     'L3_gnn_W_qkv': 3.851,
     'L3_gnn_W_o': 3.765}
    for name, (base, spread) in spreads.items():
        noise = np.random.default_rng([zlib.crc32(name.encode()), seed]).standard_normal(out[name].shape)
        drawn = base * np.exp(spread * noise) if base else spread * noise
        out[name] = jnp.asarray(drawn.astype(out[name].dtype))
    for name, factor in factors.items():
        out[name] = (out[name] * factor).astype(out[name].dtype)
    return out
```

```python
from contextlib import ExitStack

import numpy as np

import concourse.bass as bass
from concourse import mybir

ALU = mybir.AluOpType
ACT = mybir.ActivationFunctionType
F32 = mybir.dt.float32
BF16 = mybir.dt.bfloat16
I32 = mybir.dt.int32
I16 = mybir.dt.int16
AX_X = mybir.AxisListType.X

P = 128
D = 256
H = D // P
N_NODES = 6250
NT = -(-N_NODES // P)
NP = NT * P
LAST = N_NODES - (NT - 1) * P
E = 106250
NB = 32
SHIFT = 5
NBK = NP // NB + 1
FE = -(-(-(-E // P)) // 16) * 16
RING = 16
GRP = 4
NCH = -(-(P * FE // P + NBK) // RING) * RING
NG = RING // GRP
REC = 8
HEADS, HD = 8, 32
KVW = D + HEADS * (HD + 1)
R_IDX, R_LOC, R_T16, R_T32, R_W = range(5)
T16, T32, BASES = 16, 32, 8
NO_NODE = 99.0
BATCH = 16
NBATCH = FE // BATCH


class Seq:

    def __init__(self, eng, sem):
        self.eng, self.sem, self.n, self.i, self.k, self.first = eng, sem, 0, None, 0, 0

    def value(self):
        return self.n if self.i is None else self.i * self.k + (self.n - self.first * self.k)

    def link(self, ins):
        ins.then_inc(self.sem, 1)
        self.n += 1
        self.eng.wait_ge(self.sem, self.value())

    def loop(self, turns, per_turn, body):
        start = self.n
        with self.eng.Fori(0, turns) as i:
            self.i, self.k, self.first = i, per_turn, 0
            body(i)
            assert self.n - start == per_turn, (self.n - start, per_turn)
        self.i = None
        self.n = start + turns * per_turn


def walk(eng, total, unroll, lag, step, q=None, links=0):
    turns = total // unroll
    head = 2 if unroll <= 4 else 1
    assert lag <= unroll and turns > head
    for c in range(head * unroll):
        step(c, c % unroll, c // unroll)
    start = q.n if q else 0
    with eng.Fori(head, turns) as i:
        if q:
            q.i, q.k, q.first = i, links, head
        for j in range(unroll):
            step(i * unroll + j, j, i)
    if q:
        assert q.n - start == links, (q.n - start, links)
        q.i, q.n = None, start + (turns - head) * links
    for c in range(turns * unroll, total + lag):
        step(c, c % unroll, c // unroll)


def turn(i, j, lag, unroll):
    return i + (j - lag) // unroll


def past(c, n):
    return not isinstance(c, int) or c >= n


def live(c, lag, total):
    return not isinstance(c, int) or 0 <= c - lag < total


def program(nc, A, out):
    with ExitStack() as ctx:
        def sb(name, shape, dt=F32):
            return ctx.enter_context(nc.sbuf_tensor(name, shape, dt))

        def pb(name, shape=(P, 512), dt=F32):
            return ctx.enter_context(nc.psum_tensor(name, list(shape), dt))

        def sem(name):
            return ctx.enter_context(nc.semaphore(name))

        def dram(name, shape, dt=F32):
            return nc.dram_tensor(name, shape, dt, kind="Internal").ap()

        rec_dst = dram("rec_dst", (NCH * P, REC))
        rec_src = dram("rec_src", (NCH * P, REC))
        src_ix_d = dram("src_ix_d", (P, FE), I32)
        src_rec_d = dram("src_rec_d", (P, FE * REC))
        x1_d = dram("x1_d", (NP, D))
        x2_d = dram("x2_d", (NP, D))
        x3_d = dram("x3_d", (NP, D))
        att_d = dram("att_d", (NBK, P, H * (HD + 1)))
        tab_d = dram("tab_d", (2, NCH), I32)
        keep_d = dram("keep_d", (P, NCH))
        kv_d = dram("kv_d", (NP, KVW))
        bas_d = dram("bas_d", (NBK, P, H * BASES * NB))

        aggT = sb("aggT", [P, H, NBK * NB])
        nodeb = sb("nodeb", [P, NT, D])
        cntT = sb("cntT", [P, NBK * NB])
        coef = sb("coef", [P, NCH, BASES])
        rows = sb("rows", [P, RING, D])
        wreg = sb("wreg", [P, 3072])
        rec = sb("rec", [P, NG, GRP, REC])
        gidx = sb("gidx", [P, NG, GRP], I32)
        oh = sb("oh", [P, NG, GRP, NB])
        t16 = sb("t16", [P, NG, GRP, T16])
        t32 = sb("t32", [P, 2, GRP, T32])
        t32T = sb("t32T", [T32, 2, GRP * P])
        wcomp = sb("wcomp", [T32, BASES])
        ident = sb("ident", [P, P])
        ones = sb("ones", [P, P])
        before = sb("before", [P, P])
        iota = sb("iota", [P, 256])
        chunk_tab = sb("chunk_tab", [64, NCH], I32)
        bkt_i, last_i = chunk_tab[0:1, :], chunk_tab[32:33, :]
        keep = sb("keep", [P, NCH])
        small = sb("small", [P, 64])
        stg = rows[:, :, :].rearrange("p a b -> p (a b)")
        cnts = stg[:, 0:4 * NBK].rearrange("p (a b) -> p a b", a=4)
        ring_ix = sb("ring_ix", [P, 2, BATCH], I32)
        ring_rec = sb("ring_rec", [P, 2, BATCH, REC])

        flat = aggT[:, :, :].rearrange("p a b -> p (a b)")
        def part(k, n=FE):
            return flat[:, k * FE:k * FE + n]
        key_i, aux_i, bk, _, pos, _, zero, tmp = (part(k) for k in range(8))
        mask = [part(k).bitcast(BF16)[:, h * FE:(h + 1) * FE] for k in (3, 13) for h in range(2)]
        scan = [part(5), part(14)]
        wt = part(8)
        key_i, aux_i = key_i.bitcast(I32), aux_i.bitcast(I32)
        t16_i, t32_i = part(9).bitcast(I32), part(10).bitcast(I32)
        bk16 = tmp.bitcast(BF16)[:, 0:FE]
        tmp_i = part(12).bitcast(I32)
        spare = nodeb[:, :, :].rearrange("p a b -> p (a b)")
        cf = coef[:, :, :].rearrange("p a b -> p (a b)")

        def records(v):
            return v[:, 0:FE * REC].rearrange("p (f r) -> p f r", r=REC)
        after = FE * REC + FE
        assert 15 * FE <= H * NBK * NB and after + 2 * NCH <= NT * D and FE * REC <= NCH * BASES

        ps = [pb(f"ps{i}") for i in range(8)]

        s_const = sem("s_const")
        s_load = sem("s_load")
        s_fill = sem("s_fill")
        s_dve = sem("s_dve")
        s_pool = sem("s_pool")

        last_row = (E // FE)
        tail = E - last_row * FE
        assert last_row == P - 1

        class Sort:
            cleared = sem("sort_cleared")
            loaded = sem("sort_loaded")
            counted = sem("sort_counted")
            summed = sem("sort_summed")
            base = sem("sort_base")
            row = sem("sort_row")
            cols = sem("sort_cols")
            over = sem("sort_over")
            table = sem("sort_table")
            masked = sem("sort_masked")
            scanned = sem("sort_scanned")
            staged = [sem(f"sort_staged{i}") for i in range(2)]
            tabled = sem("sort_tabled")
            kept = sem("sort_kept")
            sent = [sem(f"sort_sent{i}") for i in range(2)]

            def __init__(self, nth, key, idx, dst, full, erec, pos_i, chunks, keep):
                self.key, self.idx, self.dst, self.full, self.nth = key, idx, dst, full, nth
                self.erec, self.pos_i, self.keep = erec, pos_i, keep
                self.bkt_i, self.last_i = chunks[0:1, :], chunks[32:33, :]
                self.filled = sem(f"sort{nth}_filled")

            def loads(self):
                got = [(self.key, key_i), (self.idx, aux_i)]
                if self.full:
                    got += [(A["edge_type_16"], t16_i), (A["edge_type_32"], t32_i),
                            (A["edge_weight1"].rearrange("e a -> (e a)"), wt)]
                return got

        by_dst = Sort(0, A["dst"], A["src"], rec_dst, True, records(spare), spare[:, FE * REC:after].bitcast(I32), chunk_tab, keep)
        by_src = Sort(1, A["src"], A["dst"], rec_src, False, records(cf), part(11).bitcast(I32),
                      spare[0:64, after + NCH:after + 2 * NCH].bitcast(I32), spare[:, after:after + NCH])

        def sort_sp(sp, s):
            sp.wait_ge(s.cleared, s.nth + 1)
            for arr, to in s.loads():
                sp.dma_start(to[0:last_row, :], arr[0:last_row * FE].rearrange("(p f) -> p f", f=FE)).then_inc(s.loaded, 16)
                sp.dma_start(to[last_row:P, 0:tail], arr[last_row * FE:E].rearrange("(a f) -> a f", a=1)).then_inc(s.loaded, 16)

        def sort_dve(dve, s, q, tables):
            V = nc.vector
            erec, pos_i = s.erec, s.pos_i
            n_loads = 32 * (len(s.loads()) + s.nth * len(by_dst.loads()))
            V.memset(key_i, NBK * NB - NB)
            V.memset(wt, 0.0)
            V.memset(zero, 0.0)
            V.memset(erec, 0.0)
            V.memset(t16_i, 0)
            V.memset(t32_i, 0)
            q.link(V.memset(aux_i, 0))
            dve.sem_inc(s.cleared, 1)
            dve.wait_ge(s.loaded, n_loads)
            q.link(V.tensor_scalar(tmp_i, key_i, NB - 1, None, ALU.bitwise_and))
            V.tensor_copy(erec[:, :, R_LOC], tmp_i)
            V.tensor_copy(erec[:, :, R_IDX], aux_i)
            V.tensor_copy(erec[:, :, R_T16], t16_i)
            V.tensor_copy(erec[:, :, R_T32], t32_i)
            q.link(V.tensor_copy(erec[:, :, R_W], wt))
            q.link(V.tensor_scalar(tmp_i, key_i, SHIFT, None, ALU.arith_shift_right))
            q.link(V.tensor_copy(bk, tmp_i))

            q.link(V.tensor_copy(bk16, bk))
            before_these = s.nth * 2 * NBK

            def count(b, j, i):
                if past(b, 4):
                    dve.wait_ge(s.masked, before_these + b - 3)
                V.tensor_scalar(mask[j], bk16, iota[:, bass.ds(b, 1)], None, ALU.is_equal, ALU.add,
                                accum_out=cnts[:, 0, bass.ds(b, 1)]).then_inc(s.masked, 1)
            walk(dve, NBK, 4, 0, count)
            dve.wait_ge(s.masked, before_these + NBK)
            dve.sem_inc(s.counted, 1)
            dve.wait_ge(s.summed, s.nth + 1)
            totals = cnts[:, 1, :]
            q.link(V.tensor_scalar(tmp_i[:, 0:NBK], ps[1][:, 0:NBK], float(P - 1), None, ALU.add))
            q.link(V.tensor_scalar(tmp_i[:, 0:NBK], tmp_i[:, 0:NBK], 7, None, ALU.arith_shift_right))
            q.link(V.tensor_copy(totals, tmp_i[:, 0:NBK]))
            q.link(V.tensor_scalar(totals, totals, 1.0, None, ALU.max))
            ends = cnts[:, 2, :]
            q.link(V.tensor_tensor_scan(ends, totals, zero[:, 0:NBK], 0.0, ALU.add, ALU.add))
            dve.sem_inc(s.row, 1)
            base = cnts[:, 3, :]
            q.link(V.tensor_tensor(base, ends, totals, ALU.subtract))
            q.link(V.tensor_scalar(base, base, float(P), -1.0, ALU.mult, ALU.add))
            q.link(V.tensor_tensor(base, base, ps[0][:, 0:NBK], ALU.add))

            def rank(b, j, i):
                if live(b, 2, NBK):
                    bb, jj = b - 2, (j - 2) % 4
                    dve.wait_ge(s.scanned, s.nth * NBK + bb + 1)
                    if past(bb, 1):
                        dve.wait_ge(s.base, s.nth * NBK + bb)
                    dve.sem_inc(s_fill, 1)
                    V.copy_predicated(pos, mask[jj].bitcast(I16), scan[jj % 2]).then_inc(s.base, 1)
                if live(b, 1, NBK):
                    bb, jj = b - 1, (j - 1) % 4
                    dve.wait_ge(s.masked, before_these + NBK + bb + 1)
                    if past(bb, 2):
                        dve.wait_ge(s.base, s.nth * NBK + bb - 1)
                    V.tensor_tensor_scan(scan[jj % 2], mask[jj], zero, base[:, bass.ds(bb, 1)], ALU.add, ALU.add).then_inc(s.scanned, 1)
                if live(b, 0, NBK):
                    if past(b, 4):
                        dve.wait_ge(s.base, s.nth * NBK + b - 3)
                    V.tensor_scalar(mask[j], bk16, iota[:, bass.ds(b, 1)], None, ALU.is_equal).then_inc(s.masked, 1)
            walk(dve, NBK, 4, 2, rank)
            dve.wait_ge(s.base, (s.nth + 1) * NBK)
            q.link(V.tensor_copy(pos_i, pos))
            q.link(V.tensor_scalar(tmp_i, pos_i, GRP * P - 1, None, ALU.bitwise_and))
            q.link(V.tensor_tensor(pos_i, pos_i, tmp_i, ALU.subtract))
            q.link(V.tensor_scalar(key_i, tmp_i, P - 1, 2, ALU.bitwise_and, ALU.logical_shift_left))
            q.link(V.tensor_tensor(pos_i, pos_i, key_i, ALU.add))
            q.link(V.tensor_scalar(tmp_i, tmp_i, 7, None, ALU.arith_shift_right))
            q.link(V.tensor_tensor(pos_i, pos_i, tmp_i, ALU.add))
            dve.wait_ge(s.cols, s.nth + 1)
            q.link(V.tensor_copy(small[:, 0:1], ps[2][:, 0:1]))
            q.link(V.tensor_copy(small[0:NBK - P, 1:2], ps[2][0:NBK - P, 1:2]))
            chunk_no = tables["chunk_no"]
            q.link(V.tensor_scalar(tables["over0"], chunk_no, small[:, 0:1], None, ALU.is_ge))
            q.link(V.tensor_scalar(tables["over1"][0:NBK - P], chunk_no[0:NBK - P], small[0:NBK - P, 1:2], None, ALU.is_ge))
            dve.sem_inc(s.over, 1)
            dve.wait_ge(s.table, s.nth + 1)
            for k in range(0, NCH, 512):
                n = min(512, NCH - k)
                q.link(V.tensor_scalar(bkt[:, k:k + n], ps[3 + k // 512][:, 0:n], float(NBK - 1), None, ALU.min))
            q.link(V.memset(bkt[:, NCH:NCH + 1], float(NBK)))
            V.tensor_copy(s.bkt_i, bkt[0:1, 0:NCH])
            V.tensor_tensor(s.last_i, bkt[0:1, 0:NCH], bkt[0:1, 1:NCH + 1], ALU.not_equal)
            V.memset(s.keep[:, 0:1], 0.0)
            q.link(V.tensor_tensor(s.keep[:, 1:NCH], bkt[:, 1:NCH], bkt[:, 0:NCH - 1], ALU.is_equal))
            dve.sem_inc(s.tabled, 1)

        def stage(sp, s, n, k, ix, recs, turn):
            if turn is not None:
                sp.wait_ge(s.sent[k], turn * BATCH * 16)
            sp.dma_start(ring_ix[:, k, :], ix[:, bass.ds(n * BATCH, BATCH)]).then_inc(s.staged[k], 16)
            sp.dma_start(ring_rec[:, k], recs[:, bass.ds(n * BATCH, BATCH), :]).then_inc(s.staged[k], 16)

        def send(pool, s, n, k, turn):
            pool.wait_ge(s.staged[k], 32 * (turn + 1))
            pool.sem_inc(s_pool, 1)
            for f in range(BATCH):
                nc.gpsimd.indirect_dma_start(
                    out=s.dst, out_offset=bass.IndirectOffsetOnAxis(ap=ring_ix[:, k, f:f + 1], axis=0),
                    in_=ring_rec[:, k, f, :], in_offset=None).then_inc(s.sent[k], 16)

        def sort_pe(pe, s):
            T = nc.tensor
            pe.wait_ge(s.counted, s.nth + 1)
            pe.wait_ge(s_const, 1)
            T.matmul(ps[0][:, 0:NBK], before[:, :], cnts[:, 0, :], start=True, stop=True)
            T.matmul(ps[1][:, 0:NBK], ones[:, :], cnts[:, 0, :], start=True, stop=True).then_inc(s.summed, 1)
            pe.wait_ge(s.row, s.nth + 1)
            T.matmul(ps[2][:, 0:1], cnts[0:1, 2, 0:P], ones[0:1, 0:1], start=True, stop=True)
            T.matmul(ps[2][0:NBK - P, 1:2], cnts[0:1, 2, P:NBK], ones[0:1, 0:1], start=True, stop=True).then_inc(s.cols, 1)
            pe.wait_ge(s.over, s.nth + 1)
            for k in range(0, NCH, 512):
                n = min(512, NCH - k)
                T.matmul(ps[3 + k // 512][:, 0:n], ones[:, :], tabs["over0"][:, k:k + n], start=True, stop=False)
                last = T.matmul(ps[3 + k // 512][:, 0:n], ones[0:NBK - P, :], tabs["over1"][0:NBK - P, k:k + n], start=False, stop=True)
            last.then_inc(s.table, 1)

        src_ix = src_ix_d
        src_recs = src_rec_d.rearrange("p (f r) -> p f r", r=REC)
        SENT_DST = NBATCH // 2

        def dst_stage_sp(sp):
            def step(n, k, i):
                if isinstance(n, int) and n == 2:
                    sort_sp(sp, by_src)
                stage(sp, by_dst, n, k, by_dst.pos_i, by_dst.erec, i if past(n, 2) else None)
            sp.wait_ge(by_dst.tabled, 1)
            walk(sp, NBATCH, 2, 0, step)

        def dst_send_pool(pool):
            walk(pool, NBATCH, 2, 0, lambda n, k, i: send(pool, by_dst, n, k, i))

        def src_stage(sp, n, k, i):
            stage(sp, by_src, n, k, src_ix, src_recs, SENT_DST + i)

        def src_send(pool, n, k, i):
            send(pool, by_src, n, k, SENT_DST + i)

        tabs = {"chunk_no": cntT[:, 0:NCH], "over0": cntT[:, NCH:2 * NCH], "over1": cntT[:, 2 * NCH:3 * NCH]}
        chunk_no_i = cntT[:, 3 * NCH:4 * NCH].bitcast(I32)
        empty = cntT[:, 4 * NCH:4 * NCH + 520].rearrange("p (n r) -> p n r", r=REC)
        bkt = cntT[:, 4 * NCH + 520:5 * NCH + 521]
        iota_i = cntT[:, 5 * NCH + 521:5 * NCH + 777].bitcast(I32)
        EMPTY = 65
        assert NCH * P % (EMPTY * P) == 0

        got_rec = [sem(f"got_rec{i}") for i in range(NG)]
        got_idx = sem("got_idx")
        made_oh = sem("made_oh")
        got_rows = [sem(f"got_rows{i}") for i in range(RING)]
        TURNS = NCH // RING

        l0_oh = sem("l0_oh")
        l0_mm = sem("l0_mm")
        l0_acc = sem("l0_acc")
        l0_tT = sem("l0_tT")
        l0_tS = sem("l0_tS")
        l0_look = sem("l0_look")
        l0_coef = sem("l0_coef")
        zeroed = sem("zeroed")
        wc_loaded = sem("wc_loaded")

        def load_step(sp, table, used, turns_before=0):
            src = table.rearrange("(g p a) r -> g p (a r)", p=P, a=GRP)

            def step(c, j, i):
                if j % GRP == 0 and live(c, 0, NCH):
                    g = j // GRP
                    k = i * NG + g
                    if not isinstance(c, int) or c >= RING:
                        sp.wait_ge(used, turns_before * NG + k + 1 - NG)
                    sp.dma_start(rec[:, g, :, :].rearrange("p a r -> p (a r)"),
                                 src[bass.ds(k, 1), :, :].rearrange("a p r -> (a p) r")).then_inc(got_rec[g], 16)
            return step

        def gather_rows(pool, layer, table, used, ringbuf):
            def step(c, j, i):
                g = j // GRP
                if j % GRP == 0:
                    pool.wait_ge(got_idx, (layer * TURNS + i) * NG + g + 1)
                    if not isinstance(c, int) or c >= RING:
                        pool.wait_ge(used, c + GRP - RING)
                    pool.sem_inc(s_pool, 1)
                nc.gpsimd.indirect_dma_start(
                    out=ringbuf[:, j, :], out_offset=None, in_=table,
                    in_offset=bass.IndirectOffsetOnAxis(ap=gidx[:, g, j % GRP:j % GRP + 1], axis=0)).then_inc(got_rows[j], 16)
            walk(pool, NCH, RING, 0, step)

        def group_ready(dve, c, j, i, layer, used):
            g = j // GRP
            dve.wait_ge(got_rec[g], 16 * (layer * TURNS + i + 1))
            if not isinstance(c, int) or c >= RING:
                dve.wait_ge(used, c + GRP - RING)
            nc.vector.tensor_copy(gidx[:, g, :], rec[:, g, :, R_IDX]).then_inc(got_idx, 1)
            return nc.vector.tensor_tensor(oh[:, g], iota[:, 0:NB].unsqueeze(1).broadcast_to([P, GRP, NB]),
                                           rec[:, g, :, R_LOC:R_LOC + 1].broadcast_to([P, GRP, NB]), ALU.is_equal)

        L0_LAG = 7

        def add_chunk(dve, c, bank, summed):
            b = dve.value_load(bkt_i[:, bass.ds(c, 1)], min_val=0, max_val=NBK - 1)
            at = bass.ds(b * NB, NB)
            dve.wait_ge(summed, c + 1)
            return at, nc.vector.tensor_tensor(aggT[:, :, at], aggT[:, :, at],
                                               bank[:, 0:H * NB].rearrange("p (h n) -> p h n", h=H), ALU.add)

        def l0_edges_dve(dve):
            V = nc.vector

            def step(c, j, i):
                if j % GRP == 0 and live(c, 0, NCH):
                    g = j // GRP
                    group_ready(dve, c, j, i, 0, l0_mm)
                    V.tensor_tensor(t16[:, g], iota[:, 0:T16].unsqueeze(1).broadcast_to([P, GRP, T16]),
                                    rec[:, g, :, R_T16:R_T16 + 1].broadcast_to([P, GRP, T16]), ALU.is_equal)
                    V.tensor_tensor(t32[:, g % 2], iota[:, 0:T32].unsqueeze(1).broadcast_to([P, GRP, T32]),
                                    rec[:, g, :, R_T32:R_T32 + 1].broadcast_to([P, GRP, T32]), ALU.is_equal).then_inc(l0_oh, 1)
                if live(c, L0_LAG, NCH):
                    cc, jj = c - L0_LAG, (j - L0_LAG) % RING
                    bank = ps[jj % 4]
                    at, _ = add_chunk(dve, cc, bank, l0_mm)
                    V.tensor_tensor(cntT[0:T16, at], cntT[0:T16, at], bank[0:T16, H * NB:H * NB + NB], ALU.add).then_inc(l0_acc, 1)
                    dve.wait_ge(l0_acc, cc + 1)
                    if jj % GRP == GRP - 1:
                        g = jj // GRP
                        dve.wait_ge(l0_look, turn(i, j, L0_LAG, RING) * NG + g + 1)
                        V.tensor_tensor(coef[:, bass.ds(cc - GRP + 1, GRP), :],
                                        ps[6 + g % 2][:, 0:GRP * BASES].rearrange("p (a b) -> p a b", a=GRP),
                                        rec[:, g, :, R_W:R_W + 1].broadcast_to([P, GRP, BASES]), ALU.mult).then_inc(l0_coef, 1)
            V.memset(aggT[:, :, :], 0.0)
            V.memset(cntT[0:T16, :], 0.0).then_inc(zeroed, 1)
            dve.wait_ge(zeroed, 1)
            walk(dve, NCH, RING, L0_LAG, step)

        def l0_edges_pe(pe):
            T = nc.tensor
            pe.wait_ge(wc_loaded, 16)

            def step(c, j, i):
                g = j // GRP
                k = i * NG + g
                if j % GRP == 0:
                    pe.wait_ge(l0_oh, k + 1)
                    if not isinstance(k, int) or k >= 2:
                        pe.wait_ge(l0_tS, k - 1)
                    for a in range(GRP):
                        last = T.transpose(ps[4 + g % 2][0:T32, a * P:(a + 1) * P], t32[:, g % 2, a, :], ident[:, :])
                    last.then_inc(l0_tT, 1)
                pe.wait_ge(got_rows[j], 16 * (0 * TURNS + i + 1))
                if not isinstance(c, int) or c >= 4:
                    pe.wait_ge(l0_acc, c - 3)
                bank = ps[j % 4]
                for h in range(H):
                    T.matmul(bank[:, h * NB:(h + 1) * NB], rows[:, j, h * P:(h + 1) * P], oh[:, g, j % GRP, :], start=True, stop=True)
                T.matmul(bank[0:T16, H * NB:H * NB + NB], t16[:, g, j % GRP, :], oh[:, g, j % GRP, :],
                         start=True, stop=True).then_inc(l0_mm, 1)
                if j % GRP == GRP - 1:
                    pe.wait_ge(l0_tS, k + 1)
                    if not isinstance(k, int) or k >= 2:
                        pe.wait_ge(l0_coef, k - 1)
                    for a in range(GRP):
                        last = T.matmul(ps[6 + g % 2][:, a * BASES:(a + 1) * BASES], t32T[:, g % 2, a * P:(a + 1) * P],
                                        wcomp[:, :], start=True, stop=True)
                    last.then_inc(l0_look, 1)
            walk(pe, NCH, RING, 0, step)

        def l0_edges_act(act):
            def step(c, j, i):
                if j % GRP == 0:
                    g = j // GRP
                    k = i * NG + g
                    act.wait_ge(l0_tT, k + 1)
                    if not isinstance(k, int) or k >= 2:
                        act.wait_ge(l0_look, k - 1)
                    nc.scalar.copy(t32T[:, g % 2, :], ps[4 + g % 2][0:T32, :]).then_inc(l0_tS, 1)
            walk(act, NCH, RING, 0, step)

        lns = sb("lns", [P, 3, 2, 16])
        ln = lns[:, 0]
        neg_half = sb("neg_half", [P, D])

        class Norm:

            sems = [(sem(f"norm_var{k}"), sem(f"norm_rstd{k}")) for k in range(3)]

            def __init__(self, at=0, layer=0):
                self.var, self.rstd = self.sems[at]
                self.before = layer * NT
                self.ln = lns[:, at]

            def stats(self, q, z, p, eps):
                q.link(nc.vector.bn_stats(self.ln[:, p, 0:6], z))
                q.eng.sem_inc(s_fill, 1)
                q.link(nc.vector.bn_aggr(self.ln[:, p, 6:8], self.ln[:, p, 0:6]))
                nc.vector.tensor_scalar(self.ln[:, p, 8:9], self.ln[:, p, 7:8], eps, None, ALU.add).then_inc(self.var, 1)

            def power(self, pool, n, p):
                pool.wait_ge(self.var, self.before + n)
                pool.sem_inc(s_pool, 1)
                nc.gpsimd.tensor_tensor(self.ln[:, p, 9:10], self.ln[:, p, 8:9], neg_half[:, 0:1], ALU.pow).then_inc(self.rstd, 1)

            def apply(self, dve, n, y, z, p):
                dve.wait_ge(self.rstd, self.before + n)
                return nc.vector.tensor_scalar(y, z, self.ln[:, p, 6:7], self.ln[:, p, 9:10], ALU.subtract, ALU.mult)

        def staged(at, *dims):
            n = int(np.prod(dims))
            v = stg[:, at:at + n]
            names = "abc"[:len(dims)]
            return v.rearrange(f"p ({' '.join(names)}) -> p {' '.join(names)}", **dict(zip(names, dims)))
        aggS = staged(0, 2, H, P)
        cntS = staged(512, 2, P)
        hT = staged(768, 2, H, P)
        hS = staged(1280, 2, D)
        yS = staged(1792, 2, D)
        zS = staged(2304, 2, D)
        wS = staged(2816, 2, 2 * D)
        kvS = staged(2816, 2, KVW)
        v2 = {n: wreg[:, k * 512:(k + 1) * 512].rearrange("p (h o) -> p h o", h=H) for k, n in enumerate(["wl", "wr"])}
        b_l, gamma, beta, mu = (wreg[:, 1024 + k * D:1024 + (k + 1) * D] for k in range(4))
        scl = wreg[:, 1024 + 4 * D:1024 + 5 * D]
        w0 = sem("w0")
        n0 = {k: sem(f"n0_{k}") for k in ("mm", "b", "o", "sq", "ss", "rn", "out", "sum", "mu", "sub", "sqr", "var", "ve", "pw")}
        l0_done = sem("l0_done")
        c0_out = sem("c0_out")
        c0_z = sem("c0_z")
        norm0 = Norm(0, 0)
        PIECE = 7
        assert NT % PIECE == 0 and LAST < P

        tile_in = [sem(f"tile_in{p}") for p in range(2)]
        tile_out = [sem(f"tile_out{p}") for p in range(2)]
        TILES = [(NT + 1) // 2, NT // 2]

        def loads_before(walk_name, p):
            per_tile = {"n0": 48, "c0": 16, "n1": 48, "n2": 32, "n3": 32}
            names = list(per_tile)
            return TILES[p] * sum(per_tile[n] for n in names[:names.index(walk_name)])

        def tile_rows(t):
            return bass.ds(t * P, P)

        def n0_sp(sp):
            def step(t, p, i):
                if not isinstance(t, int) or t >= 2:
                    sp.wait_ge(n0["mm"], t - 1)
                sp.dma_start(aggS[:, p], aggT[:, :, tile_rows(t)]).then_inc(tile_in[p], 16)
                sp.dma_start(cntS[0:T16, p], cntT[0:T16, tile_rows(t)]).then_inc(tile_in[p], 16)
                sp.dma_start(hT[:, p], A["xT"].rearrange("(h p) n -> p h n", p=P)[:, :, tile_rows(t)]).then_inc(tile_in[p], 16)
            sp.wait_ge(l0_done, 1)
            walk(sp, NT, 2, 0, step)

            def again(t, p, i):
                if live(t, 0, NT):
                    if not isinstance(t, int) or t >= 2:
                        sp.wait_ge(c0_z, t - 1)
                    sp.dma_start(hS[:, p], A["x"][tile_rows(t), :]).then_inc(tile_in[p], 16)
                if live(t, 1, NT):
                    sp.wait_ge(c0_out, t)
                    sp.dma_start(x1_d[tile_rows(t - 1), :], yS[:, 1 - p]).then_inc(tile_out[1 - p], 16)
            sp.wait_ge(n0["mm"], NT)
            walk(sp, NT, 2, 1, again)
            sp.wait_ge(tile_out[0], 16 * 1 * TILES[0])
            sp.wait_ge(tile_out[1], 16 * 1 * TILES[1])
            sp.sem_inc(x1_ready, 1)

        def n0_pe(pe):
            T = nc.tensor
            pe.wait_ge(w0, 16 * 5)

            def step(t, p, i):
                pe.wait_ge(tile_in[p], loads_before("n0", p) + 48 * (i + 1))
                if not isinstance(t, int) or t >= 2:
                    pe.wait_ge(n0["o"], t - 1)
                for h in range(H):
                    T.matmul(ps[p][:, 0:D], aggS[:, p, h, :], v2["wl"][:, h, :], start=(h == 0), stop=(h == H - 1))
                T.matmul(ps[p][:, D:D + 1], cntS[0:T16, p, :], ones[0:T16, 0:1], start=True, stop=True)
                for h in range(H):
                    T.matmul(ps[2 + p][:, 0:D], hT[:, p, h, :], v2["wr"][:, h, :], start=(h == 0), stop=False)
                T.matmul(ps[2 + p][:, 0:D], ones[0:1, :], b_l[0:1, :], start=False, stop=True).then_inc(n0["mm"], 1)
            walk(pe, NT, 2, 0, step)
            pe.wait_ge(n0["out"], NT)
            for t in range(NT):
                n = LAST if t == NT - 1 else P
                last = T.matmul(ps[4][:, 0:D], ones[0:n, :], nodeb[0:n, t, :], start=(t == 0), stop=(t == NT - 1))
            last.then_inc(n0["sum"], 1)
            for k in range(NT // PIECE):
                pe.wait_ge(n0["sqr"], k + 1)
                for t in range(k * PIECE, (k + 1) * PIECE):
                    n = LAST if t == NT - 1 else P
                    last = T.matmul(ps[5][:, 0:D], ones[0:n, :], sq_of(t)[0:n, :], start=(t == 0), stop=(t == NT - 1))
                last.then_inc(n0["var"], 1)

        def sq_of(t):
            return flat[:, ((t // PIECE) % 2 * PIECE + t % PIECE) * D:((t // PIECE) % 2 * PIECE + t % PIECE + 1) * D]

        def n0_act(act):
            S = nc.scalar

            def step(t, p, i):
                act.wait_ge(n0["mm"], t + 1)
                if not isinstance(t, int) or t >= 2:
                    act.wait_ge(n0["o"], t - 1)
                S.copy(zS[:, p], ps[2 + p][:, 0:D]).then_inc(n0["b"], 1)
                act.wait_ge(n0["o"], t + 1)
                S.activation(wS[:, p, 0:D], yS[:, p], ACT.Square, accum_out=ln[:, p, 0:1]).then_inc(n0["sq"], 1)
            walk(act, NT, 2, 0, step)
            for k in range(NT // PIECE):
                act.wait_ge(n0["sub"], k + 1)
                if k >= 2:
                    act.wait_ge(n0["var"], k - 1)
                S.activation(flat[:, k % 2 * PIECE * D:(k % 2 + 1) * PIECE * D],
                             nodeb[:, k * PIECE:(k + 1) * PIECE, :].rearrange("p t d -> p (t d)"), ACT.Square).then_inc(n0["sqr"], 1)

        def n0_pool(pool):
            def step(t, p, i):
                pool.wait_ge(n0["ss"], t + 1)
                pool.sem_inc(s_pool, 1)
                nc.gpsimd.tensor_tensor(ln[:, p, 2:3], ln[:, p, 1:2], neg_half[:, 0:1], ALU.pow).then_inc(n0["rn"], 1)
            walk(pool, NT, 2, 0, step)
            pool.wait_ge(n0["ve"], 1)
            nc.gpsimd.tensor_tensor(scl, scl, neg_half[:, :], ALU.pow).then_inc(n0["pw"], 1)
            walk(pool, NT, 2, 0, lambda t, p, i: norm0.power(pool, t + 1, p))

        def n0_dve(dve, q):
            V = nc.vector

            def step(t, p, i):
                if live(t, 0, NT):
                    dve.wait_ge(n0["b"], t + 1)
                    if not isinstance(t, int) or t >= 2:
                        dve.wait_ge(n0["out"], t - 1)
                    q.link(V.tensor_scalar(ln[:, p, 4:5], ps[p][:, D:D + 1], 1.0, None, ALU.max))
                    q.link(V.reciprocal(ln[:, p, 5:6], ln[:, p, 4:5]))
                    V.scalar_tensor_tensor(out=yS[:, p], in0=ps[p][:, 0:D], scalar=ln[:, p, 5:6], in1=zS[:, p],
                                           op0=ALU.mult, op1=ALU.add).then_inc(n0["o"], 1)
                    dve.wait_ge(n0["sq"], t + 1)
                    V.tensor_scalar(ln[:, p, 1:2], ln[:, p, 0:1], 1e-24, None, ALU.max).then_inc(n0["ss"], 1)
                if live(t, 1, NT):
                    dve.wait_ge(n0["rn"], t)
                    V.tensor_scalar(nodeb[:, bass.ds(t - 1, 1), :].rearrange("p a d -> p (a d)"), yS[:, 1 - p],
                                    ln[:, 1 - p, 2:3], None, ALU.mult).then_inc(n0["out"], 1)
            walk(dve, NT, 2, 1, step, q, 4)
            dve.wait_ge(n0["sum"], 1)
            q.link(V.tensor_scalar(mu, ps[4][:, 0:D], 1.0 / N_NODES, None, ALU.mult))
            for k in range(NT // PIECE):
                piece = nodeb[:, k * PIECE:(k + 1) * PIECE, :]
                V.tensor_tensor(piece, piece, mu.unsqueeze(1).broadcast_to([P, PIECE, D]), ALU.subtract).then_inc(n0["sub"], 1)
            dve.wait_ge(n0["var"], NT // PIECE)
            V.tensor_scalar(scl, ps[5][:, 0:D], 1.0 / N_NODES, 1e-5, ALU.mult, ALU.add).then_inc(n0["ve"], 1)
            dve.wait_ge(n0["pw"], 1)
            q.link(V.tensor_tensor(scl, scl, gamma, ALU.mult))

            def again(t, p, i):
                if live(t, 0, NT):
                    if not isinstance(t, int) or t >= 2:
                        dve.wait_ge(c0_out, t - 1)
                    q.link(V.tensor_tensor(zS[:, p], nodeb[:, bass.ds(t, 1), :].rearrange("p a d -> p (a d)"), scl, ALU.mult))
                    q.link(V.tensor_tensor(zS[:, p], zS[:, p], beta, ALU.add))
                    dve.wait_ge(tile_in[p], loads_before("c0", p) + 16 * (i + 1))
                    V.scalar_tensor_tensor(out=zS[:, p], in0=zS[:, p], scalar=0.0, in1=hS[:, p],
                                           op0=ALU.max, op1=ALU.add).then_inc(c0_z, 1)
                    dve.wait_ge(c0_z, t + 1)
                    norm0.stats(q, zS[:, p], p, 1e-5)
                if live(t, 1, NT):
                    pp = 1 - p
                    if not isinstance(t, int) or t >= 3:
                        dve.wait_ge(tile_out[pp], 16 * 0 * TILES[pp] + 16 * turn(i, p, 1, 2))
                    norm0.apply(dve, t, yS[:, pp], zS[:, pp], pp).then_inc(c0_out, 1)
            walk(dve, NT, 2, 1, again, q, 8)

        x1_ready = sem("x1_ready")
        x2_ready = sem("x2_ready")
        l1_mm, l1_acc, l1_done, l1_zero = (sem(f"l1_{k}") for k in ("mm", "acc", "done", "zero"))
        L1_LAG = 7

        def l1_edges_dve(dve):
            def step(c, j, i):
                if j % GRP == 0 and live(c, 0, NCH):
                    group_ready(dve, c, j, i, 1, l1_mm).then_inc(made_oh, 1)
                if live(c, L1_LAG, NCH):
                    cc = c - L1_LAG
                    _, add = add_chunk(dve, cc, ps[(j - L1_LAG) % 8], l1_mm)
                    add.then_inc(l1_acc, 1)
                    dve.wait_ge(l1_acc, cc + 1)
            nc.vector.memset(aggT[:, :, :], 0.0).then_inc(l1_zero, 1)
            dve.wait_ge(l1_zero, 1)
            walk(dve, NCH, RING, L1_LAG, step)
            dve.sem_inc(l1_done, 1)

        def l1_edges_pe(pe):
            def step(c, j, i):
                g = j // GRP
                if j % GRP == 0:
                    pe.wait_ge(made_oh, i * NG + g + 1)
                pe.wait_ge(got_rows[j], 16 * (1 * TURNS + i + 1))
                if past(c, 8):
                    pe.wait_ge(l1_acc, c - 7)
                for h in range(H):
                    last = nc.tensor.matmul(ps[j % 8][:, h * NB:(h + 1) * NB], rows[:, j, h * P:(h + 1) * P],
                                            oh[:, g, j % GRP, :], start=True, stop=True)
                last.then_inc(l1_mm, 1)
            walk(pe, NCH, RING, 0, step)

        nodef = nodeb[:, :, :].rearrange("p a b -> p (a b)")
        wih = wreg[:, 0:1536].rearrange("p (h o) -> p h o", h=H)
        whh = wreg[:, 1536:3072].rearrange("p (h o) -> p h o", h=H)
        relW = nodef[0:T16 + 2, 0:3 * D]
        bhn = nodef[0:1, 3 * D:4 * D]
        relT = nodef[:, 4 * D:4 * D + H * T16].rearrange("p (h r) -> p h r", h=H)
        w1 = sem("w1")
        n1 = {k: sem(f"n1_{k}") for k in ("rel", "relw", "tr", "hT", "mm", "rz", "pre", "n", "y", "out")}
        norm1 = Norm(0, 1)

        def n1_sp(sp):
            def step(t, p, i):
                if live(t, 0, NT):
                    if not isinstance(t, int) or t >= 2:
                        sp.wait_ge(n1["y"], t - 1)
                    sp.dma_start(aggS[:, p], aggT[:, :, tile_rows(t)]).then_inc(tile_in[p], 16)
                    sp.dma_start(cntS[0:T16, p], cntT[0:T16, tile_rows(t)]).then_inc(tile_in[p], 16)
                    sp.dma_start(hS[:, p], x1_d[tile_rows(t), :]).then_inc(tile_in[p], 16)
                if live(t, 2, NT):
                    sp.wait_ge(n1["out"], t - 1)
                    sp.dma_start(x2_d[tile_rows(t - 2), :], yS[:, p]).then_inc(tile_out[p], 16)
            sp.wait_ge(l1_done, 1)
            walk(sp, NT, 2, 2, step)
            sp.wait_ge(tile_out[0], 16 * 2 * TILES[0])
            sp.wait_ge(tile_out[1], 16 * 2 * TILES[1])
            sp.sem_inc(x2_ready, 1)

        def n1_pe(pe):
            T = nc.tensor
            pe.wait_ge(w1, 16 * 8)
            for k in range(2):
                n = 512 if k == 0 else 256
                for h in range(H):
                    last = T.matmul(ps[6 + k][0:T16, 0:n], relT[:, h, :], wih[:, h, k * 512:k * 512 + n], start=(h == 0), stop=(h == H - 1))
            last.then_inc(n1["rel"], 1)
            pe.wait_ge(n1["relw"], 1)

            def step(t, p, i):
                rz, ih = ps[p], ps[2 + p]
                pe.wait_ge(tile_in[p], loads_before("n1", p) + 48 * (i + 1))
                if not isinstance(t, int) or t >= 2:
                    pe.wait_ge(n1["hT"], t - 1)
                for h in range(H):
                    last = T.transpose(ps[4 + p][:, h * P:(h + 1) * P], hS[:, p, h * P:(h + 1) * P], ident[:, :])
                last.then_inc(n1["tr"], 1)
                if not isinstance(t, int) or t >= 2:
                    pe.wait_ge(n1["pre"], t - 1)
                for h in range(H):
                    T.matmul(rz[:, :], aggS[:, p, h, :], wih[:, h, 0:512], start=(h == 0), stop=False)
                T.matmul(rz[:, :], cntS[0:T16 + 2, p, :], relW[:, 0:512], start=False, stop=False)
                for h in range(H):
                    T.matmul(ih[:, 0:D], aggS[:, p, h, :], wih[:, h, 512:768], start=(h == 0), stop=False)
                T.matmul(ih[:, 0:D], cntS[0:T16 + 2, p, :], relW[:, 512:768], start=False, stop=True)
                pe.wait_ge(n1["hT"], t + 1)
                for h in range(H):
                    T.matmul(rz[:, :], hT[:, p, h, :], whh[:, h, 0:512], start=False, stop=(h == H - 1))
                for h in range(H):
                    T.matmul(ih[:, D:2 * D], hT[:, p, h, :], whh[:, h, 512:768], start=(h == 0), stop=False)
                T.matmul(ih[:, D:2 * D], ones[0:1, :], bhn, start=False, stop=True).then_inc(n1["mm"], 1)
            walk(pe, NT, 2, 0, step)

        def n1_act(act):
            S = nc.scalar
            act.wait_ge(n1["rel"], 1)
            S.copy(relW[0:T16, 0:512], ps[6][0:T16, 0:512])
            S.copy(relW[0:T16, 512:768], ps[7][0:T16, 0:256]).then_inc(n1["relw"], 1)

            def step(t, p, i):
                act.wait_ge(n1["tr"], t + 1)
                if not isinstance(t, int) or t >= 2:
                    act.wait_ge(n1["mm"], t - 1)
                S.copy(hT[:, p], ps[4 + p][:, 0:D].rearrange("p (h n) -> p h n", h=H)).then_inc(n1["hT"], 1)
                act.wait_ge(n1["mm"], t + 1)
                if not isinstance(t, int) or t >= 2:
                    act.wait_ge(n1["y"], t - 1)
                S.activation(wS[:, p], ps[p][:, :], ACT.Sigmoid).then_inc(n1["rz"], 1)
                act.wait_ge(n1["pre"], t + 1)
                if not isinstance(t, int) or t >= 2:
                    act.wait_ge(tile_out[p], 16 * 1 * TILES[p] + 16 * i)
                S.activation(yS[:, p], zS[:, p], ACT.Tanh).then_inc(n1["n"], 1)
            walk(act, NT, 2, 0, step)

        def n1_pool(pool, q):
            G = nc.gpsimd

            def step(t, p, i):
                if live(t, 0, NT):
                    pool.wait_ge(n1["n"], t + 1)
                    q.link(G.tensor_tensor(zS[:, p], hS[:, p], yS[:, p], ALU.subtract))
                    q.link(G.tensor_tensor(zS[:, p], zS[:, p], wS[:, p, D:2 * D], ALU.mult))
                    q.link(G.tensor_tensor(zS[:, p], zS[:, p], yS[:, p], ALU.add))
                    G.tensor_tensor(zS[:, p], zS[:, p], hS[:, p], ALU.add).then_inc(n1["y"], 1)
                if live(t, 1, NT):
                    norm1.power(pool, t, 1 - p)
            walk(pool, NT, 2, 1, step, q, 6)

        def n1_dve(dve, q):
            V = nc.vector

            def step(t, p, i):
                if live(t, 1, NT):
                    dve.wait_ge(n1["y"], t)
                    norm1.stats(q, zS[:, 1 - p], 1 - p, 1e-5)
                if live(t, 2, NT):
                    norm1.apply(dve, t - 1, yS[:, p], zS[:, p], p).then_inc(n1["out"], 1)
                if live(t, 0, NT):
                    dve.wait_ge(n1["rz"], t + 1)
                    if not isinstance(t, int) or t >= 2:
                        dve.wait_ge(n1["out"], t - 1)
                    q.link(V.tensor_tensor(zS[:, p], wS[:, p, 0:D], ps[2 + p][:, D:2 * D], ALU.mult))
                    V.tensor_tensor(zS[:, p], zS[:, p], ps[2 + p][:, 0:D], ALU.add).then_inc(n1["pre"], 1)
            walk(dve, NT, 2, 2, step, q, 6)

        flushed = [sem(f"flushed{i}") for i in range(4)]
        l2_w, l2_mm, l2_cur, l2_zero = (sem(f"l2_{k}") for k in ("w", "mm", "cur", "zero"))
        wts = nodef[:, 0:1024].rearrange("p (s n b) -> p s n b", s=4, b=BASES)
        cur = nodef[:, 1024:3072].rearrange("p (s f) -> p s f", s=4)
        FLUSH_LAG = 16

        def flush_step(sp, sums, to, done):
            def step(c, j, i):
                if live(c, FLUSH_LAG, NCH):
                    cc, k = c - FLUSH_LAG, (j - FLUSH_LAG) % 4
                    b = sp.value_load(bkt_i[:, bass.ds(cc, 1)], min_val=0, max_val=NBK - 1)
                    is_last = sp.value_load(last_i[:, bass.ds(cc, 1)], min_val=0, max_val=1)
                    sp.wait_ge(done, cc + 1)
                    sp.dma_start(to[bass.ds(b, 1), :, :].rearrange("a p f -> (a p) f"), sums[:, k, :], cond=is_last).then_inc(flushed[k], 16)
            return step

        def l2_edges_dve(dve):
            V = nc.vector

            def step(c, j, i):
                if j % GRP == 0 and live(c, 0, NCH):
                    group_ready(dve, c, j, i, 2, l2_mm).then_inc(made_oh, 1)
                if live(c, L2_LEAD, NCH):
                    cc, jj = c - L2_LEAD, (j - L2_LEAD) % RING
                    g = jj // GRP
                    if jj % GRP == 0:
                        dve.wait_ge(made_oh, (TURNS + turn(i, j, L2_LEAD, RING)) * NG + g + 1)
                    if past(cc, 4):
                        dve.wait_ge(l2_mm, cc - 3)
                    V.tensor_tensor(wts[:, jj % 4], oh[:, g, jj % GRP, :].unsqueeze(2).broadcast_to([P, NB, BASES]),
                                    coef[:, bass.ds(cc, 1), :].broadcast_to([P, NB, BASES]), ALU.mult).then_inc(l2_w, 1)
                if live(c, L2_LAG, NCH):
                    cc, k = c - L2_LAG, (j - L2_LAG) % 4
                    if past(cc, 1):
                        dve.wait_ge(l2_cur, cc)
                    dve.wait_ge(l2_mm, cc + 1)
                    if past(c, 4 + L2_LAG):
                        dve.wait_ge(flushed[k], 16 * (i * (RING // 4) + (j - L2_LAG) // 4))
                    V.scalar_tensor_tensor(out=cur[:, k], in0=cur[:, (k - 1) % 4], scalar=keep[:, bass.ds(cc, 1)],
                                           in1=ps[(j - L2_LAG) % 8][:, :], op0=ALU.mult, op1=ALU.add).then_inc(l2_cur, 1)
            V.memset(cur, 0.0).then_inc(l2_zero, 1)
            dve.wait_ge(l2_zero, 1)
            walk(dve, NCH, RING, L2_LAG, step)

        L2_LEAD, L2_LAG = 5, 8

        def l2_edges_pe(pe):
            def step(c, j, i):
                pe.wait_ge(l2_w, c + 1)
                pe.wait_ge(got_rows[j], 16 * (2 * TURNS + i + 1))
                if past(c, 8):
                    pe.wait_ge(l2_cur, c - 7)
                for h in range(H):
                    last = nc.tensor.matmul(ps[j % 8][:, :].rearrange("p (n h b) -> p n h b", n=NB, h=H)[:, :, h, :],
                                            rows[:, j, h * P:(h + 1) * P], wts[:, j % 4], start=True, stop=True)
                last.then_inc(l2_mm, 1)
            walk(pe, NCH, RING, 0, step)

        bases = cntT[:, 0:4096].rearrange("p (b h o) -> p b h o", b=BASES, h=H)
        wkv = cntT[:, 4096:5120].rearrange("p (h o) -> p h o", h=H)
        wq = cntT[:, 5120:5632].rearrange("p (h o) -> p h o", h=H)
        basS = nodef[:, 3072:7168].rearrange("p (s n h b) -> p s n h b", s=2, h=H, b=BASES)
        w2 = sem("w2")
        n2 = {k: sem(f"n2_{k}") for k in ("ones", "mm", "z", "out", "tr", "xT", "kv", "kvS")}
        n2_kvst = [sem(f"n2_kvst{p}") for p in range(2)]
        norm2 = Norm(0, 2)
        QT = aggT

        def n2_sp(sp):
            def step(t, p, i):
                if live(t, 0, NT):
                    if not isinstance(t, int) or t >= 2:
                        sp.wait_ge(n2["z"], t - 1)
                    sp.dma_start(nodef[:, 3072 + p * 2048:3072 + (p + 1) * 2048].rearrange("p (q f) -> p q f", q=4),
                                 bas_d[bass.ds(4 * t, 4), :, :].rearrange("q p f -> p q f")).then_inc(tile_in[p], 16)
                    sp.dma_start(hS[:, p], x2_d[tile_rows(t), :]).then_inc(tile_in[p], 16)
                    src_stage(sp, t + 2, p, i + 1)
                if live(t, 1, NT):
                    sp.wait_ge(n2["out"], t)
                    sp.dma_start(x3_d[tile_rows(t - 1), :], yS[:, 1 - p]).then_inc(tile_out[1 - p], 16)
                if live(t, 2, NT):
                    sp.wait_ge(n2["kvS"], t - 1)
                    sp.dma_start(kv_d[tile_rows(t - 2), :], kvS[:, p]).then_inc(n2_kvst[p], 16)
            for k in range(4):
                sp.wait_ge(flushed[k], 16 * (NCH // 4))
            walk(sp, NT, 2, 2, step)
            src_stage(sp, NBATCH - 1, 1, NBATCH // 2 - 1)
            for p in range(2):
                sp.wait_ge(tile_out[p], 16 * 3 * TILES[p])
                sp.wait_ge(n2_kvst[p], 16 * TILES[p])
                sp.wait_ge(by_src.sent[p], 2 * SENT_DST * BATCH * 16)
            sp.sem_inc(x3_ready, 1)
        x3_ready = sem("x3_ready")

        def n2_pe(pe):
            T = nc.tensor
            pe.wait_ge(w2, 16 * 3)

            def step(t, p, i):
                if live(t, 0, NT):
                    pe.wait_ge(tile_in[p], loads_before("n2", p) + 32 * (i + 1))
                    if not isinstance(t, int) or t >= 2:
                        pe.wait_ge(n2["z"], t - 1)
                    for k in range(BASES * H):
                        last = T.matmul(ps[p][:, 0:D], basS[:, p, :, k % H, k // H], bases[:, k // H, k % H, :],
                                        start=(k == 0), stop=(k == BASES * H - 1))
                    last.then_inc(n2["mm"], 1)
                if live(t, 1, NT):
                    pe.wait_ge(n2["out"], t)
                    if not isinstance(t, int) or t >= 3:
                        pe.wait_ge(n2["xT"], t - 2)
                    for h in range(H):
                        last = T.transpose(ps[2 + 1 - p][:, h * P:(h + 1) * P], yS[:, 1 - p, h * P:(h + 1) * P], ident[:, :])
                    last.then_inc(n2["tr"], 1)
                if live(t, 2, NT):
                    pe.wait_ge(n2["xT"], t - 1)
                    if not isinstance(t, int) or t >= 4:
                        pe.wait_ge(n2["kvS"], t - 3)
                    for h in range(H):
                        T.matmul(ps[4 + p][:, :], hT[:, p, h, :], wkv[:, h, :], start=(h == 0), stop=(h == H - 1))
                    for o in range(H):
                        for h in range(H):
                            last = T.matmul(ps[6 + p][:, o * P:(o + 1) * P], wq[:, h, o * P:(o + 1) * P], hT[:, p, h, :],
                                            start=(h == 0), stop=(h == H - 1))
                    last.then_inc(n2["kv"], 1)
            walk(pe, NT, 2, 2, step)

        def n2_act(act):
            S = nc.scalar
            act.wait_ge(n2["ones"], 1)

            def step(t, p, i):
                if live(t, 2, NT):
                    act.wait_ge(n2["kv"], t - 1)
                    if not isinstance(t, int) or t >= 4:
                        act.wait_ge(n2_kvst[p], 16 * turn(i, p, 2, 2))
                    S.copy(QT[:, :, tile_rows(t - 2)], ps[6 + p][:, 0:D].rearrange("p (h n) -> p h n", h=H))
                    S.copy(kvS[:, p, 0:D], ps[4 + p][:, 0:D])
                    S.copy(kvS[:, p, D:KVW].rearrange("p (m e) -> p m e", m=HEADS)[:, :, 0:HD],
                           ps[4 + p][:, D:2 * D].rearrange("p (m e) -> p m e", m=HEADS)).then_inc(n2["kvS"], 1)
                if live(t, 1, NT):
                    act.wait_ge(n2["tr"], t)
                    if not isinstance(t, int) or t >= 3:
                        act.wait_ge(n2["kv"], t - 2)
                    S.copy(hT[:, 1 - p], ps[2 + 1 - p][:, 0:D].rearrange("p (h n) -> p h n", h=H)).then_inc(n2["xT"], 1)
            walk(act, NT, 2, 2, step)

        def n2_dve(dve, q):
            V = nc.vector
            dve.wait_ge(l2_cur, NCH)
            for p in range(2):
                last = V.memset(kvS[:, p, D:KVW].rearrange("p (m e) -> p m e", m=HEADS)[:, :, HD:HD + 1], 1.0)
            last.then_inc(n2["ones"], 1)

            def step(t, p, i):
                if live(t, 0, NT):
                    dve.wait_ge(n2["mm"], t + 1)
                    if not isinstance(t, int) or t >= 2:
                        dve.wait_ge(n2["out"], t - 1)
                    V.scalar_tensor_tensor(out=zS[:, p], in0=ps[p][:, 0:D], scalar=0.0, in1=hS[:, p],
                                           op0=ALU.max, op1=ALU.add).then_inc(n2["z"], 1)
                    dve.wait_ge(n2["z"], t + 1)
                    norm2.stats(q, zS[:, p], p, 1e-5)
                if live(t, 1, NT):
                    pp = 1 - p
                    if not isinstance(t, int) or t >= 3:
                        dve.wait_ge(tile_out[pp], 16 * 2 * TILES[pp] + 16 * turn(i, p, 1, 2))
                        dve.wait_ge(n2["tr"], t - 2)
                    norm2.apply(dve, t, yS[:, pp], zS[:, pp], pp).then_inc(n2["out"], 1)
            walk(dve, NT, 2, 1, step, q, 4)

        HH = HEADS // H
        assert HH * NB == P and HH * HD == P and NB == HD == 32
        SCALE = float(HD) ** -0.5
        MASKED = 2.0 ** 100
        FRESH, FLOOR = -1e20, -0.9e20
        AW = H * (HD + 1)
        qbd = nodef[:, 3072:4096].rearrange("p (s h m n) -> p s h m n", s=4, h=H, m=HH)
        kT = nodef[:, 512:1024].rearrange("p (s h e) -> p s h e", s=2, h=H)
        ohT = nodef[0:NB + 1, 1024:1152].bitcast(BF16).rearrange("p (s e) -> p s e", s=2)
        off = nodef[0:NB + 1, 1152:1216].bitcast(BF16)
        prob = nodef[:, 1280:1792].rearrange("p (s h e) -> p s h e", s=2, h=H)
        probT = nodef[:, 1792:2304].rearrange("p (s h e) -> p s h e", s=2, h=H)
        acc = nodef[:, 2304:2304 + 4 * AW].rearrange("p (s f) -> p s f", s=4)
        st = nodef[:, 2600:2680].rearrange("p (s k h) -> p s k h", s=8, k=5)
        M_NEW, M_PREV, M_CHUNK, M_NEG, M_DIFF = range(5)
        corr = nodef[:, 2680:2696].rearrange("p (s h) -> p s h", s=8)
        oh3 = nodef[:, 2696:2952].bitcast(BF16).rearrange("p (g a n) -> p g a n", g=NG, a=GRP)
        identb = nodef[:, 2952:3016].bitcast(BF16)
        bmask = small[:, 8:8 + HH]
        rows3 = cf[:, 0:RING * KVW].rearrange("p (s f) -> p s f", s=RING)
        l3 = {k: sem(f"l3_{k}") for k in ("a", "q", "k", "s", "m", "exp", "ptr", "pt", "pv", "acc", "init")}
        tabs_back = sem("tabs_back")
        AT_K, AT_S, AT_M, AT_PTR, AT_PT, AT_PV, AT_ACC = 1, 2, 3, 4, 5, 6, 7
        LEAD = 5

        def l3_edges_dve(dve, q):
            V = nc.vector
            dve.wait_ge(tabs_back, 48)
            q.link(V.tensor_scalar(keep[:, :], keep[:, :], -FRESH, FRESH, ALU.mult, ALU.add))
            V.memset(st[:, :, :, :], FLOOR)
            V.tensor_copy(identb, ident[:, :])
            for m in range(HH):
                V.tensor_scalar(off[0:NB, m * NB:(m + 1) * NB], ident[0:NB, 0:NB], MASKED, None, ALU.mult)
            V.memset(off[NB:NB + 1, :], -MASKED)
            V.memset(ohT[NB:NB + 1, :, :], 1.0)
            q.link(V.memset(acc[:, :, :], 0.0))
            dve.sem_inc(l3["init"], 1)

            def step(c, j, i):
                g = j // GRP
                if live(c, LEAD + AT_ACC, NCH):
                    cc, p, k = c - LEAD - AT_ACC, (j - LEAD - AT_ACC) % 2, (j - LEAD - AT_ACC) % 4
                    if past(cc, 1):
                        dve.wait_ge(l3["acc"], cc)
                    dve.wait_ge(l3["pv"], cc + 1)
                    if past(cc, 4):
                        dve.wait_ge(flushed[k], 16 * (NCH // 4 + i * (RING // 4) + (j - LEAD - AT_ACC) // 4))
                    for h in range(H):
                        at = slice(h * (HD + 1), (h + 1) * (HD + 1))
                        last = V.scalar_tensor_tensor(out=acc[:, k, at], in0=acc[:, (k - 1) % 4, at],
                                                      scalar=corr[:, (j - LEAD - AT_ACC) % 8, h:h + 1], in1=ps[6 + p][:, at],
                                                      op0=ALU.mult, op1=ALU.add)
                    last.then_inc(l3["acc"], 1)
                if live(c, LEAD + AT_M, NCH):
                    cc, p, k = c - LEAD - AT_M, (j - LEAD - AT_M) % 2, (j - LEAD - AT_M) % 8
                    dve.wait_ge(l3["s"], cc + 1)
                    V.tensor_reduce(st[:, k, M_CHUNK], ps[2 + p][:, 0:D].rearrange("p (h e) -> p h e", h=H), AX_X, ALU.max)
                    q.link(V.tensor_scalar(st[:, k, M_PREV], st[:, (k - 1) % 8, M_NEW], keep[:, bass.ds(cc, 1)], None, ALU.add))
                    q.link(V.scalar_tensor_tensor(out=st[:, k, M_NEW], in0=st[:, k, M_CHUNK], scalar=FLOOR, in1=st[:, k, M_PREV],
                                                  op0=ALU.max, op1=ALU.max))
                    V.tensor_scalar(st[:, k, M_NEG], st[:, k, M_NEW], -SCALE, None, ALU.mult)
                    V.tensor_tensor(st[:, k, M_DIFF], st[:, k, M_PREV], st[:, k, M_NEW], ALU.subtract).then_inc(l3["m"], 1)
                if j % GRP == 0 and live(c, 0, NCH):
                    dve.wait_ge(got_rec[g], 16 * (3 * TURNS + i + 1))
                    if past(c, RING):
                        dve.wait_ge(l3["a"], c + GRP - RING)
                    V.tensor_copy(gidx[:, g, :], rec[:, g, :, R_IDX]).then_inc(got_idx, 1)
                    V.tensor_tensor(oh3[:, g], iota[:, 0:NB].unsqueeze(1).broadcast_to([P, GRP, NB]),
                                    rec[:, g, :, R_LOC:R_LOC + 1].broadcast_to([P, GRP, NB]), ALU.is_equal).then_inc(made_oh, 1)
                if live(c, LEAD, NCH):
                    cc = c - LEAD
                    b = dve.value_load(bkt_i[:, bass.ds(cc, 1)], min_val=0, max_val=NBK - 1)
                    if past(cc, 4):
                        dve.wait_ge(l3["s"], cc - 3)
                    V.tensor_tensor(qbd[:, (j - LEAD) % 4], QT[:, :, bass.ds(b * NB, NB)].unsqueeze(2).broadcast_to([P, H, HH, NB]),
                                    bmask.unsqueeze(1).unsqueeze(3).broadcast_to([P, H, HH, NB]), ALU.mult).then_inc(l3["q"], 1)
            walk(dve, NCH, RING, LEAD + AT_ACC, step, q, 2 * RING)

        def l3_edges_act(act):
            S = nc.scalar
            act.wait_ge(l3["init"], 1)

            def step(c, j, i):
                if live(c, AT_K, NCH):
                    cc, p = c - AT_K, (j - AT_K) % 2
                    act.wait_ge(l3["a"], cc + 1)
                    if past(cc, 2):
                        act.wait_ge(l3["s"], cc - 1)
                    S.copy(kT[:, p], ps[p][:, 0:D].rearrange("p (h e) -> p h e", h=H))
                    S.copy(ohT[0:NB, p], ps[p][0:NB, D:D + P]).then_inc(l3["k"], 1)
                if live(c, AT_PT, NCH):
                    cc, p = c - AT_PT, (j - AT_PT) % 2
                    act.wait_ge(l3["ptr"], cc + 1)
                    if past(cc, 2):
                        act.wait_ge(l3["pv"], cc - 1)
                    S.copy(probT[:, p], ps[4 + p][:, 0:D].rearrange("p (h e) -> p h e", h=H)).then_inc(l3["pt"], 1)
                if live(c, AT_M, NCH):
                    cc, p, k = c - AT_M, (j - AT_M) % 2, (j - AT_M) % 8
                    act.wait_ge(l3["m"], cc + 1)
                    if past(cc, 2):
                        act.wait_ge(l3["ptr"], cc - 1)
                    if past(cc, 8):
                        act.wait_ge(l3["acc"], cc - 7)
                    for h in range(H):
                        S.activation(prob[:, p, h], ps[2 + p][:, h * P:(h + 1) * P], ACT.Exp, bias=st[:, k, M_NEG, h:h + 1], scale=SCALE)
                    S.activation(corr[:, k], st[:, k, M_DIFF], ACT.Exp, scale=SCALE).then_inc(l3["exp"], 1)
            walk(act, NCH, RING, AT_PT, step)

        def l3_edges_pe(pe):
            T = nc.tensor
            pe.wait_ge(l3["init"], 1)

            def step(c, j, i):
                g = j // GRP
                if live(c, AT_PV, NCH):
                    cc, p, jj = c - AT_PV, (j - AT_PV) % 2, (j - AT_PV) % RING
                    pe.wait_ge(l3["pt"], cc + 1)
                    if past(cc, 2):
                        pe.wait_ge(l3["acc"], cc - 1)
                    for h in range(H):
                        for m in range(HH):
                            v = D + (h * HH + m) * (HD + 1)
                            last = T.matmul(ps[6 + p][m * NB:(m + 1) * NB, h * (HD + 1):(h + 1) * (HD + 1)],
                                            probT[:, p, h, m * NB:(m + 1) * NB], rows3[:, jj, v:v + HD + 1], start=True, stop=True)
                    last.then_inc(l3["pv"], 1)
                if live(c, AT_PTR, NCH):
                    cc, p = c - AT_PTR, (j - AT_PTR) % 2
                    pe.wait_ge(l3["exp"], cc + 1)
                    if past(cc, 2):
                        pe.wait_ge(l3["pt"], cc - 1)
                    for h in range(H):
                        last = T.transpose(ps[4 + p][:, h * P:(h + 1) * P], prob[:, p, h], ident[:, :])
                    last.then_inc(l3["ptr"], 1)
                if live(c, AT_S, NCH):
                    cc, p = c - AT_S, (j - AT_S) % 2
                    pe.wait_ge(l3["k"], cc + 1)
                    pe.wait_ge(l3["q"], cc + 1)
                    if past(cc, 2):
                        pe.wait_ge(l3["exp"], cc - 1)
                    T.matmul(ps[2 + p][:, 0:D].rearrange("p (h e) -> p h e", h=H), off,
                             ohT[:, p].unsqueeze(1).broadcast_to([NB + 1, H, P]), start=True, stop=False)
                    for h in range(H):
                        last = T.matmul(ps[2 + p][:, h * P:(h + 1) * P], qbd[:, (j - AT_S) % 4, h].rearrange("p m n -> p (m n)"),
                                        kT[:, p, h], start=False, stop=(h == H - 1))
                    last.then_inc(l3["s"], 1)
                if live(c, 0, NCH):
                    pe.wait_ge(got_rows[j], 16 * (3 * TURNS + i + 1))
                    if j % GRP == 0:
                        pe.wait_ge(made_oh, (2 * TURNS + i) * NG + g + 1)
                    if past(c, 2):
                        pe.wait_ge(l3["k"], c - 1)
                    for h in range(H):
                        T.transpose(ps[j % 2][:, h * P:(h + 1) * P], rows3[:, j, h * P:(h + 1) * P], ident[:, :])
                    T.matmul(ps[j % 2][0:NB, D:D + P], oh3[:, g, j % GRP, :], identb, start=True, stop=True).then_inc(l3["a"], 1)
            walk(pe, NCH, RING, AT_PV, step)

        wo = cntT[:, 0:512].rearrange("p (h o) -> p h o", h=H)
        wi = cntT[:, 512:2560].rearrange("p (h o) -> p h o", h=H)
        wout = cntT[:, 2560:4608].rearrange("p (k o) -> p k o", k=8)
        g1, b1, g2, b2 = (cntT[:, 4608 + k * D:4608 + (k + 1) * D] for k in range(4))
        attS = nodef[:, 3072:3072 + 8 * AW].rearrange("p (s q f) -> p s q f", s=2, q=4)
        attN = nodef[:, 3600:4112].rearrange("p (s h q e) -> p s h q e", s=2, h=H, q=4)
        attT = nodef[:, 4112:4624].rearrange("p (s f) -> p s f", s=2)
        rden = nodef[:, 4624:4640].rearrange("p (s q h) -> p s q h", s=2, q=4)
        xin = nodef[:, 4640:5664].rearrange("p (s d) -> p s d", s=4)
        pre = nodef[:, 5664:6688].rearrange("p (s d) -> p s d", s=4)
        preT = nodef[:, 6688:7200].rearrange("p (s h n) -> p s h n", s=2, h=H)
        inT = nodef[:, 7200:9248].rearrange("p (s k n) -> p s k n", s=2, k=8)
        w3 = sem("w3")
        n3 = {k: sem(f"n3_{k}") for k in ("att", "o", "pre", "ptr", "pT", "i", "g", "o2", "z3", "out")}
        norms = [Norm(0, 3), Norm(1), Norm(2)]
        U3 = 4
        AT_O, AT_PRE, AT_I, AT_END = 1, 1, 2, 3

        def n3_sp(sp):
            def step(t, j, i):
                p = j % 2
                if live(t, 0, NT):
                    if past(t, 2):
                        sp.wait_ge(n3["att"], t - 1)
                    sp.dma_start(attS[:, p], att_d[bass.ds(4 * t, 4), :, :].rearrange("q p f -> p q f")).then_inc(tile_in[p], 16)
                    if past(t, 4):
                        sp.wait_ge(n3["z3"], t - 3)
                    sp.dma_start(xin[:, j], x3_d[tile_rows(t), :]).then_inc(tile_in[p], 16)
                if live(t, AT_END, NT):
                    p = (j - AT_END) % 2
                    sp.wait_ge(n3["out"], t - AT_END + 1)
                    if isinstance(t, int) and t - AT_END == NT - 1:
                        sp.dma_start(out[N_NODES - LAST:N_NODES, :], yS[0:LAST, p]).then_inc(tile_out[p], 16)
                    else:
                        sp.dma_start(out[tile_rows(t - AT_END), :], yS[:, p]).then_inc(tile_out[p], 16)
            for k in range(4):
                sp.wait_ge(flushed[k], 16 * 2 * (NCH // 4))
            walk(sp, NT, U3, AT_END, step)
            sp.wait_ge(tile_out[0], 16 * 4 * TILES[0])
            sp.wait_ge(tile_out[1], 16 * 4 * TILES[1])

        def n3_pe(pe):
            T = nc.tensor
            pe.wait_ge(w3, 16 * 7)

            def step(t, j, i):
                if live(t, AT_I, NT):
                    tt, jj, p = t - AT_I, (j - AT_I) % 4, (j - AT_I) % 2
                    pe.wait_ge(n3["pre"], tt + 1)
                    if past(tt, 1):
                        pe.wait_ge(n3["pT"], tt)
                    for h in range(H):
                        last = T.transpose(ps[2][:, h * P:(h + 1) * P], pre[:, jj, h * P:(h + 1) * P], ident[:, :])
                    last.then_inc(n3["ptr"], 1)
                if live(t, AT_O, NT):
                    tt, p = t - AT_O, (j - AT_O) % 2
                    pe.wait_ge(n3["att"], tt + 1)
                    if past(tt, 2):
                        pe.wait_ge(n3["pre"], tt - 1)
                    for h in range(H):
                        last = T.matmul(ps[p][:, 0:D], attT[:, p, h * P:(h + 1) * P], wo[:, h, :], start=(h == 0), stop=(h == H - 1))
                    last.then_inc(n3["o"], 1)
                if live(t, AT_END, NT):
                    tt, p = t - AT_END, (j - AT_END) % 2
                    pe.wait_ge(n3["g"], tt + 1)
                    if past(tt, 1):
                        pe.wait_ge(n3["z3"], tt)
                    for k in range(8):
                        last = T.matmul(ps[3][:, 0:D], inT[:, p, k], wout[:, k, :], start=(k == 0), stop=(k == 7))
                    last.then_inc(n3["o2"], 1)
                if live(t, AT_I, NT):
                    tt, p = t - AT_I, (j - AT_I) % 2
                    pe.wait_ge(n3["pT"], tt + 1)
                    if past(tt, 2):
                        pe.wait_ge(n3["g"], tt - 1)
                    for k in range(8):
                        for h in range(H):
                            last = T.matmul(ps[4 + 2 * p + k // 4][:, k % 4 * P:(k % 4 + 1) * P], wi[:, h, k * P:(k + 1) * P], preT[:, p, h],
                                            start=(h == 0), stop=(h == H - 1))
                    last.then_inc(n3["i"], 1)
            walk(pe, NT, U3, AT_END, step)

        def n3_act(act):
            S = nc.scalar

            def step(t, j, i):
                if live(t, AT_I, NT):
                    tt, p = t - AT_I, (j - AT_I) % 2
                    act.wait_ge(n3["ptr"], tt + 1)
                    if past(tt, 2):
                        act.wait_ge(n3["i"], tt - 1)
                    S.copy(preT[:, p], ps[2][:, 0:D].rearrange("p (h n) -> p h n", h=H)).then_inc(n3["pT"], 1)
                    act.wait_ge(n3["i"], tt + 1)
                    if past(tt, 2):
                        act.wait_ge(n3["o2"], tt - 1)
                    for k in range(2):
                        last = S.activation(inT[:, p, k * 4:(k + 1) * 4], ps[4 + 2 * p + k][:, :].rearrange("p (k n) -> p k n", k=4), ACT.Gelu)
                    last.then_inc(n3["g"], 1)
            walk(act, NT, U3, AT_END, step)

        def n3_dve(dve, q):
            V = nc.vector

            def normed(norm, n, y, z, p, eps):
                norm.stats(q, z, p, eps)
                q.link(norm.apply(dve, n, y, z, p))

            def step(t, j, i):
                if live(t, 0, NT):
                    p = j % 2
                    dve.wait_ge(tile_in[p], loads_before("n3", p) + 32 * (i * (U3 // 2) + j // 2 + 1))
                    heads = attS[:, p].rearrange("p q (h e) -> p q h e", h=H)
                    q.link(V.tensor_scalar(rden[:, p], heads[:, :, :, HD], 1e-30, None, ALU.max))
                    q.link(V.reciprocal(rden[:, p], rden[:, p]))
                    q.link(V.tensor_tensor(attN[:, p].rearrange("p h q e -> p q h e"), heads[:, :, :, 0:HD],
                                           rden[:, p].unsqueeze(3).broadcast_to([P, 4, H, HD]), ALU.mult))
                    if past(t, 2):
                        dve.wait_ge(n3["o"], t - 1)
                    V.transpose(attT[:, p], attN[:, p].rearrange("p h q e -> p (h q e)")).then_inc(n3["att"], 1)
                if live(t, AT_PRE, NT):
                    tt, jj, p = t - AT_PRE, (j - AT_PRE) % 4, (j - AT_PRE) % 2
                    dve.wait_ge(n3["o"], tt + 1)
                    q.link(V.tensor_tensor(zS[:, p], ps[p][:, 0:D], xin[:, jj], ALU.add))
                    normed(norms[0], tt + 1, zS[:, p], zS[:, p], p, 1e-12)
                    q.link(V.tensor_tensor(zS[:, p], zS[:, p], g1, ALU.mult))
                    if past(tt, 4):
                        dve.wait_ge(n3["z3"], tt - 3)
                    V.tensor_tensor(pre[:, jj], zS[:, p], b1, ALU.add).then_inc(n3["pre"], 1)
                if live(t, AT_END, NT):
                    tt, jj, p = t - AT_END, (j - AT_END) % 4, (j - AT_END) % 2
                    dve.wait_ge(n3["o2"], tt + 1)
                    dve.wait_ge(n3["pre"], tt + 1)
                    z = wS[:, p, 0:D]
                    q.link(V.tensor_tensor(z, ps[3][:, 0:D], pre[:, jj], ALU.add))
                    normed(norms[1], tt + 1, z, z, p, 1e-12)
                    q.link(V.tensor_tensor(z, z, g2, ALU.mult))
                    q.link(V.tensor_tensor(z, z, b2, ALU.add))
                    V.tensor_tensor(z, z, xin[:, jj], ALU.add).then_inc(n3["z3"], 1)
                    dve.wait_ge(n3["z3"], tt + 1)
                    norms[2].stats(q, z, p, 1e-5)
                    if past(tt, 2):
                        dve.wait_ge(tile_out[p], 16 * 3 * TILES[p] + 16 * (i * (U3 // 2) + (j - AT_END) // 2))
                    norms[2].apply(dve, tt + 1, yS[:, p], z, p).then_inc(n3["out"], 1)
                    dve.wait_ge(n3["out"], tt + 1)
            walk(dve, NT, U3, AT_END, step, q, U3 * 16)

        def n3_pool(pool):
            def step(t, j, i):
                if live(t, AT_PRE, NT):
                    norms[0].power(pool, t - AT_PRE + 1, (j - AT_PRE) % 2)
                if live(t, AT_END, NT):
                    norms[1].power(pool, t - AT_END + 1, (j - AT_END) % 2)
                    norms[2].power(pool, t - AT_END + 1, (j - AT_END) % 2)
            walk(pool, NT, U3, AT_END, step)

        block = ctx.enter_context(nc.Block())

        @block.sync
        def _(sp):
            sp.dma_start(wcomp[:, :], A["L2_gnn_w_comp"]).then_inc(wc_loaded, 16)
            sp.dma_start(v2["wl"], A["W_lT"].rearrange("(h p) o -> p h o", p=P)).then_inc(w0, 16)
            sp.dma_start(v2["wr"], A["W_rT"].rearrange("(h p) o -> p h o", p=P)).then_inc(w0, 16)
            for to, name in ((b_l, "L0_gnn_b_l"), (gamma, "L0_gnn_gamma"), (beta, "L0_gnn_beta")):
                sp.dma_start(to, A[name].partition_broadcast(P)).then_inc(w0, 16)
            sp.wait_ge(s_const, 1)
            for s in (by_dst, by_src):
                sp.dma_start(s.dst.rearrange("(p m e) r -> p m (e r)", p=P, e=EMPTY),
                             empty.rearrange("p n r -> p (n r)").unsqueeze(1).broadcast_to([P, NCH // EMPTY, EMPTY * REC])).then_inc(s.filled, 16)
            sort_sp(sp, by_dst)
            dst_stage_sp(sp)
            sp.wait_ge(by_src.tabled, 2)
            sp.dma_start(tab_d[0:1, :], by_src.bkt_i).then_inc(by_src.kept, 16)
            sp.dma_start(tab_d[1:2, :], by_src.last_i).then_inc(by_src.kept, 16)
            sp.dma_start(keep_d, by_src.keep).then_inc(by_src.kept, 16)
            sp.dma_start(src_ix_d, by_src.pos_i).then_inc(by_src.kept, 16)
            sp.dma_start(src_recs, by_src.erec).then_inc(by_src.kept, 16)
            sp.wait_ge(by_src.kept, 16 * 5)
            for k in range(2):
                sp.wait_ge(by_dst.sent[k], SENT_DST * BATCH * 16)
            walk(sp, NCH, RING, 0, load_step(sp, rec_dst, l0_coef))
            for k in range(2):
                src_stage(sp, k, k, 0)
            n0_sp(sp)
            sp.dma_start(wih, A["w_ihT"].rearrange("(h p) o -> p h o", p=P)).then_inc(w1, 16)
            sp.dma_start(whh, A["w_hhT"].rearrange("(h p) o -> p h o", p=P)).then_inc(w1, 16)
            sp.dma_start(relT, A["relT"].rearrange("(h p) r -> p h r", p=P)).then_inc(w1, 16)
            sp.dma_start(relW[T16:T16 + 1, :], A["L1_gnn_b_ih"].rearrange("(a n) -> a n", a=1)).then_inc(w1, 16)
            b_hh = A["L1_gnn_b_hh"].rearrange("(a n) -> a n", a=1)
            sp.dma_start(relW[T16 + 1:T16 + 2, 0:2 * D], b_hh[:, 0:2 * D]).then_inc(w1, 16)
            sp.dma_start(bhn, b_hh[:, 2 * D:3 * D]).then_inc(w1, 16)
            sp.dma_start(relW[T16 + 1:T16 + 2, 2 * D:3 * D], A["zeros"].rearrange("(a n) -> a n", a=1)).then_inc(w1, 16)
            walk(sp, NCH, RING, 0, load_step(sp, rec_dst, made_oh))
            sp.wait_ge(l1_done, 1)
            sp.dma_start(cntS[T16:T16 + 2, :, :], ones[0:2, :].unsqueeze(1).broadcast_to([2, 2, P])).then_inc(w1, 16)
            n1_sp(sp)
            sp.dma_start(bases, A["L2_gnn_bases"].rearrange("b (h p) o -> p b h o", p=P)).then_inc(w2, 16)
            sp.dma_start(wkv, A["W_kv"].rearrange("(h p) o -> p h o", p=P)).then_inc(w2, 16)
            sp.dma_start(wq, A["W_q"].rearrange("(h p) o -> p h o", p=P)).then_inc(w2, 16)
            load = load_step(sp, rec_dst, made_oh, TURNS)
            flush = flush_step(sp, cur, bas_d, l2_cur)

            def both(c, j, i):
                load(c, j, i)
                flush(c, j, i)
            walk(sp, NCH, RING, FLUSH_LAG, both)
            n2_sp(sp)
            sp.dma_start(bkt_i, tab_d[0:1, :]).then_inc(tabs_back, 16)
            sp.dma_start(last_i, tab_d[1:2, :]).then_inc(tabs_back, 16)
            sp.dma_start(keep[:, :], keep_d).then_inc(tabs_back, 16)
            sp.dma_start(wo, A["L3_gnn_W_o"].rearrange("(h p) o -> p h o", p=P)).then_inc(w3, 16)
            sp.dma_start(wi, A["L3_gnn_W_i"].rearrange("(h p) o -> p h o", p=P)).then_inc(w3, 16)
            sp.dma_start(wout, A["L3_gnn_W_out2"].rearrange("(k p) o -> p k o", p=P)).then_inc(w3, 16)
            for to, name in ((g1, "L3_gnn_ln1_g"), (b1, "L3_gnn_ln1_b"), (g2, "L3_gnn_ln2_g"), (b2, "L3_gnn_ln2_b")):
                sp.dma_start(to, A[name].partition_broadcast(P)).then_inc(w3, 16)
            sp.wait_ge(tabs_back, 48)
            load3 = load_step(sp, rec_src, made_oh, 2 * TURNS)
            flush3 = flush_step(sp, acc, att_d, l3["acc"])

            def both3(c, j, i):
                load3(c, j, i)
                flush3(c, j, i)
            walk(sp, NCH, RING, FLUSH_LAG, both3)
            n3_sp(sp)

        @block.gpsimd
        def _(pool):
            G = nc.gpsimd
            q = Seq(pool, sem("q_pool"))
            q.link(G.memset(ident[:, :], 0.0))
            q.link(G.affine_select(out=ident[:, :], in_=ident[:, :], compare_op=ALU.not_equal, fill=1.0,
                                   base=0, pattern=[[-1, P]], channel_multiplier=1))
            q.link(G.memset(before[:, :], 0.0))
            q.link(G.affine_select(out=before[:, :], in_=before[:, :], compare_op=ALU.is_ge, fill=1.0,
                                   base=0, pattern=[[-1, P]], channel_multiplier=1))
            q.link(G.memset(ones[:, :], 1.0))
            q.link(G.memset(neg_half[:, :], -0.5))
            q.link(G.iota(iota_i, [[1, 256]], base=0, channel_multiplier=0))
            q.link(G.tensor_copy(iota[:, :], iota_i))
            q.link(G.iota(chunk_no_i, [[1, NCH]], base=0, channel_multiplier=0))
            q.link(G.tensor_copy(tabs["chunk_no"], chunk_no_i))
            q.link(G.memset(empty, 0.0))
            q.link(G.memset(empty[:, :, R_LOC:R_LOC + 1], NO_NODE))
            q.link(G.memset(empty[:, :, R_T16:R_T32 + 1], NO_NODE))
            q.link(G.memset(bmask, 1.0))
            q.link(G.affine_select(out=bmask, in_=bmask, compare_op=ALU.is_ge, fill=0.0,
                                   base=0, pattern=[[-HD, HH]], channel_multiplier=1))
            q.link(G.affine_select(out=bmask, in_=bmask, compare_op=ALU.is_ge, fill=0.0,
                                   base=HD - 1, pattern=[[HD, HH]], channel_multiplier=-1))
            pool.sem_inc(s_const, 1)
            for s in (by_dst, by_src):
                pool.wait_ge(s.filled, 16)
            dst_send_pool(pool)
            gather_rows(pool, 0, A["x"], l0_mm, rows)
            for k in range(2):
                src_send(pool, k, k, 0)
            n0_pool(pool)
            pool.wait_ge(x1_ready, 1)
            gather_rows(pool, 1, x1_d, l1_mm, rows)
            n1_pool(pool, q)
            pool.wait_ge(x2_ready, 1)
            gather_rows(pool, 2, x2_d, l2_mm, rows)

            def n2_pool(t, p, i):
                norm2.power(pool, t + 1, p)
                src_send(pool, t + 2, p, i + 1)
            walk(pool, NT, 2, 0, n2_pool)
            src_send(pool, NBATCH - 1, 1, NBATCH // 2 - 1)
            pool.wait_ge(x3_ready, 1)
            gather_rows(pool, 3, kv_d, l3["pv"], rows3)
            n3_pool(pool)

        @block.vector
        def _(dve):
            q = Seq(dve, s_dve)
            dve.wait_ge(s_const, 1)
            sort_dve(dve, by_dst, q, tabs)
            sort_dve(dve, by_src, q, tabs)
            dve.wait_ge(by_src.kept, 16 * 5)
            for s in (by_dst, by_src):
                dve.wait_ge(s.filled, 16)
            l0_edges_dve(dve)
            dve.wait_ge(l0_acc, NCH)
            dve.sem_inc(l0_done, 1)
            dve.wait_ge(w0, 16 * 5)
            n0_dve(dve, q)
            l1_edges_dve(dve)
            n1_dve(dve, q)
            l2_edges_dve(dve)
            n2_dve(dve, q)
            dve.wait_ge(x3_ready, 1)
            l3_edges_dve(dve, q)
            dve.wait_ge(w3, 16 * 7)
            n3_dve(dve, q)

        @block.tensor
        def _(pe):
            sort_pe(pe, by_dst)
            sort_pe(pe, by_src)
            l0_edges_pe(pe)
            n0_pe(pe)
            l1_edges_pe(pe)
            n1_pe(pe)
            l2_edges_pe(pe)
            n2_pe(pe)
            l3_edges_pe(pe)
            n3_pe(pe)

        @block.scalar
        def _(act):
            l0_edges_act(act)
            n0_act(act)
            n1_act(act)
            n2_act(act)
            l3_edges_act(act)
            n3_act(act)


def kernel(**inputs):
    import numpy as _np
    import concourse.bacc as _bacc
    from concourse import mybir as _mybir
    from concourse.bass_utils import run_bass_kernel_spmd as _run

    nc = _bacc.Bacc("TRN2", target_bir_lowering=False, num_devices=1)
    arrays, args = {}, {}

    def give(name, a):
        a = _np.ascontiguousarray(a)
        arrays[f"in_{name}_dram"] = a
        args[name] = nc.dram_tensor(f"in_{name}_dram", a.shape, _mybir.dt.from_np(a.dtype), kind="ExternalInput").ap()

    for name in ["src", "dst", "edge_type_16", "edge_type_32", "edge_weight1", "L2_gnn_w_comp",
                 "L1_gnn_b_ih", "L1_gnn_b_hh", "L2_gnn_bases", "L3_gnn_W_o", "L3_gnn_W_i", "L3_gnn_W_out2", "L3_gnn_ln1_g", "L3_gnn_ln1_b",
                 "L3_gnn_ln2_g", "L3_gnn_ln2_b", "L0_gnn_b_l", "L0_gnn_gamma", "L0_gnn_beta"]:
        give(name, inputs[name])
    x = _np.asarray(inputs["x"])
    xp = _np.zeros((NP, D), x.dtype)
    xp[:N_NODES] = x
    give("x", xp)
    give("xT", xp.T)
    give("zeros", _np.zeros(D, x.dtype))
    give("w_ihT", _np.asarray(inputs["L1_gnn_w_ih"]).T)
    give("w_hhT", _np.asarray(inputs["L1_gnn_w_hh"]).T)
    give("relT", _np.asarray(inputs["L1_gnn_relvectors"]).T)
    qkv = _np.asarray(inputs["L3_gnn_W_qkv"]).reshape(D, 8, 3, 32)
    give("W_q", qkv[:, :, 0].reshape(D, D))
    give("W_kv", _np.concatenate([qkv[:, :, 1].reshape(D, D), qkv[:, :, 2].reshape(D, D)], axis=1))
    give("W_lT", _np.asarray(inputs["L0_gnn_W_l"]).T)
    give("W_rT", _np.asarray(inputs["L0_gnn_W_r"]).T)
    out = nc.dram_tensor("out_0_dram", (N_NODES, D), F32, kind="ExternalOutput").ap()
    program(nc, args, out)
    r = _run(nc, [arrays], core_ids=[0])
    return r.results[0]["out_0_dram"]
```
